# Optimizing a Trainium2 kernel written in Bass

```python
import numpy as np
import jax
import jax.numpy as jnp

def _softmax(x, axis=-1):
    return jax.nn.softmax(x, axis=axis)

def _gelu(x):
    return jax.nn.gelu(x, approximate=True)

def _silu(x):
    return jax.nn.silu(x)

def _sigmoid(x):
    return jax.nn.sigmoid(x)

def _layernorm(x, axis=-1, eps=1e-05):
    m = jnp.mean(x, axis=axis, keepdims=True)
    v = jnp.var(x, axis=axis, keepdims=True)
    return (x - m) / jnp.sqrt(v + eps)

def _scatter_add(tgt, idx, src, axis=0):
    return tgt.at[idx].add(src)

def _segment_sum(src, seg, n):
    return jax.ops.segment_sum(src, seg, n)
kernel_name = 'mk_dlrm_tower_d1_rec_r8_d5a166'

def setup_inputs(seed: int=0):
    np.random.seed(seed)
    _w = jnp.asarray

    def _rec_inputs():
        import jax
        import jax.numpy as jnp
        _tk = jax.random.key(seed)
        dense_ctx = jax.random.normal(jax.random.fold_in(_tk, 190), (512, 16), jnp.float32)
        ids = jnp.stack([jax.random.randint(jax.random.fold_in(_tk, 200 + f), (512,), 0, v, jnp.int32) for f, v in enumerate([125000, 1000, 1000, 1250, 1000, 125000, 12500, 12500, 12500, 125000, 12500, 1000, 1000, 12500, 1250, 1250, 1000, 1000, 1000, 1250, 12500, 1000, 1250, 1250, 1250, 1250, 1250, 12500, 1000, 1250, 1000, 1000, 1000, 1250, 1250, 1250, 1250, 1250, 1250, 1000])], axis=1)
        tbl_0 = 0.05 * jax.random.normal(jax.random.fold_in(_tk, 500 + 0), (125000, 64), jnp.float32)
        tbl_1 = 0.05 * jax.random.normal(jax.random.fold_in(_tk, 500 + 1), (1000, 64), jnp.float32)
        tbl_2 = 0.05 * jax.random.normal(jax.random.fold_in(_tk, 500 + 2), (1000, 64), jnp.float32)
        tbl_3 = 0.05 * jax.random.normal(jax.random.fold_in(_tk, 500 + 3), (1250, 64), jnp.float32)
        tbl_4 = 0.05 * jax.random.normal(jax.random.fold_in(_tk, 500 + 4), (1000, 64), jnp.float32)
        tbl_5 = 0.05 * jax.random.normal(jax.random.fold_in(_tk, 500 + 5), (125000, 64), jnp.float32)
        tbl_6 = 0.05 * jax.random.normal(jax.random.fold_in(_tk, 500 + 6), (12500, 64), jnp.float32)
        tbl_7 = 0.05 * jax.random.normal(jax.random.fold_in(_tk, 500 + 7), (12500, 64), jnp.float32)
        tbl_8 = 0.05 * jax.random.normal(jax.random.fold_in(_tk, 500 + 8), (12500, 64), jnp.float32)
        tbl_9 = 0.05 * jax.random.normal(jax.random.fold_in(_tk, 500 + 9), (125000, 64), jnp.float32)
        tbl_10 = 0.05 * jax.random.normal(jax.random.fold_in(_tk, 500 + 10), (12500, 64), jnp.float32)
        tbl_11 = 0.05 * jax.random.normal(jax.random.fold_in(_tk, 500 + 11), (1000, 64), jnp.float32)
        tbl_12 = 0.05 * jax.random.normal(jax.random.fold_in(_tk, 500 + 12), (1000, 64), jnp.float32)
        tbl_13 = 0.05 * jax.random.normal(jax.random.fold_in(_tk, 500 + 13), (12500, 64), jnp.float32)
        tbl_14 = 0.05 * jax.random.normal(jax.random.fold_in(_tk, 500 + 14), (1250, 64), jnp.float32)
        tbl_15 = 0.05 * jax.random.normal(jax.random.fold_in(_tk, 500 + 15), (1250, 64), jnp.float32)
        tbl_16 = 0.05 * jax.random.normal(jax.random.fold_in(_tk, 500 + 16), (1000, 64), jnp.float32)
        tbl_17 = 0.05 * jax.random.normal(jax.random.fold_in(_tk, 500 + 17), (1000, 64), jnp.float32)
        tbl_18 = 0.05 * jax.random.normal(jax.random.fold_in(_tk, 500 + 18), (1000, 64), jnp.float32)
        tbl_19 = 0.05 * jax.random.normal(jax.random.fold_in(_tk, 500 + 19), (1250, 64), jnp.float32)
        tbl_20 = 0.05 * jax.random.normal(jax.random.fold_in(_tk, 500 + 20), (12500, 64), jnp.float32)
        tbl_21 = 0.05 * jax.random.normal(jax.random.fold_in(_tk, 500 + 21), (1000, 64), jnp.float32)
        tbl_22 = 0.05 * jax.random.normal(jax.random.fold_in(_tk, 500 + 22), (1250, 64), jnp.float32)
        tbl_23 = 0.05 * jax.random.normal(jax.random.fold_in(_tk, 500 + 23), (1250, 64), jnp.float32)
        tbl_24 = 0.05 * jax.random.normal(jax.random.fold_in(_tk, 500 + 24), (1250, 64), jnp.float32)
        tbl_25 = 0.05 * jax.random.normal(jax.random.fold_in(_tk, 500 + 25), (1250, 64), jnp.float32)
        tbl_26 = 0.05 * jax.random.normal(jax.random.fold_in(_tk, 500 + 26), (1250, 64), jnp.float32)
        tbl_27 = 0.05 * jax.random.normal(jax.random.fold_in(_tk, 500 + 27), (12500, 64), jnp.float32)
        tbl_28 = 0.05 * jax.random.normal(jax.random.fold_in(_tk, 500 + 28), (1000, 64), jnp.float32)
        tbl_29 = 0.05 * jax.random.normal(jax.random.fold_in(_tk, 500 + 29), (1250, 64), jnp.float32)
        tbl_30 = 0.05 * jax.random.normal(jax.random.fold_in(_tk, 500 + 30), (1000, 64), jnp.float32)
        tbl_31 = 0.05 * jax.random.normal(jax.random.fold_in(_tk, 500 + 31), (1000, 64), jnp.float32)
        tbl_32 = 0.05 * jax.random.normal(jax.random.fold_in(_tk, 500 + 32), (1000, 64), jnp.float32)
        tbl_33 = 0.05 * jax.random.normal(jax.random.fold_in(_tk, 500 + 33), (1250, 64), jnp.float32)
        tbl_34 = 0.05 * jax.random.normal(jax.random.fold_in(_tk, 500 + 34), (1250, 64), jnp.float32)
        tbl_35 = 0.05 * jax.random.normal(jax.random.fold_in(_tk, 500 + 35), (1250, 64), jnp.float32)
        tbl_36 = 0.05 * jax.random.normal(jax.random.fold_in(_tk, 500 + 36), (1250, 64), jnp.float32)
        tbl_37 = 0.05 * jax.random.normal(jax.random.fold_in(_tk, 500 + 37), (1250, 64), jnp.float32)
        tbl_38 = 0.05 * jax.random.normal(jax.random.fold_in(_tk, 500 + 38), (1250, 64), jnp.float32)
        tbl_39 = 0.05 * jax.random.normal(jax.random.fold_in(_tk, 500 + 39), (1000, 64), jnp.float32)
        _rk = jax.random.fold_in(_tk, 7)
        W_top1 = 0.0354441 * jax.random.normal(jax.random.fold_in(_tk, 801), (796, 512), jnp.float32)
        W_top2 = 0.0441942 * jax.random.normal(jax.random.fold_in(_tk, 802), (512, 256), jnp.float32)
        W_top3 = 0.0625 * jax.random.normal(jax.random.fold_in(_tk, 803), (256, 1), jnp.float32)
        b_top1 = jnp.zeros((512,), jnp.float32)
        b_top2 = jnp.zeros((256,), jnp.float32)
        return (dense_ctx, ids, tbl_0, tbl_1, tbl_2, tbl_3, tbl_4, tbl_5, tbl_6, tbl_7, tbl_8, tbl_9, tbl_10, tbl_11, tbl_12, tbl_13, tbl_14, tbl_15, tbl_16, tbl_17, tbl_18, tbl_19, tbl_20, tbl_21, tbl_22, tbl_23, tbl_24, tbl_25, tbl_26, tbl_27, tbl_28, tbl_29, tbl_30, tbl_31, tbl_32, tbl_33, tbl_34, tbl_35, tbl_36, tbl_37, tbl_38, tbl_39, W_top1, b_top1, W_top2, b_top2, W_top3)
    dense_ctx, ids, tbl_0, tbl_1, tbl_2, tbl_3, tbl_4, tbl_5, tbl_6, tbl_7, tbl_8, tbl_9, tbl_10, tbl_11, tbl_12, tbl_13, tbl_14, tbl_15, tbl_16, tbl_17, tbl_18, tbl_19, tbl_20, tbl_21, tbl_22, tbl_23, tbl_24, tbl_25, tbl_26, tbl_27, tbl_28, tbl_29, tbl_30, tbl_31, tbl_32, tbl_33, tbl_34, tbl_35, tbl_36, tbl_37, tbl_38, tbl_39, W_top1, b_top1, W_top2, b_top2, W_top3 = _rec_inputs()

    def _L0_rec_setup():
        import jax, jax.numpy as jnp
        import numpy as np

        def _pair_indices(num_fields):
            i_idx, j_idx = np.triu_indices(num_fields, k=1)
            return (jnp.asarray(i_idx), jnp.asarray(j_idx))
        key = jax.random.key(seed)
        k1, k2 = jax.random.split(key)
        B, F, D = (256, 40, 64)
        P = F * (F - 1) // 2
        x = jax.random.normal(k1, (B, F, D), dtype=jnp.float32)
        W = jax.random.normal(k2, (P, D, D), dtype=jnp.float32) * (1.0 / np.sqrt(D))
        return {'x': x, 'W': W}
    _L0_rec_all = _L0_rec_setup()
    _L0_rec_in = {k: v for k, v in _L0_rec_all.items() if k in ('W',)}
    del _L0_rec_all
    return {'dense_ctx': dense_ctx, 'ids': ids, 'tbl_0': tbl_0, 'tbl_1': tbl_1, 'tbl_2': tbl_2, 'tbl_3': tbl_3, 'tbl_4': tbl_4, 'tbl_5': tbl_5, 'tbl_6': tbl_6, 'tbl_7': tbl_7, 'tbl_8': tbl_8, 'tbl_9': tbl_9, 'tbl_10': tbl_10, 'tbl_11': tbl_11, 'tbl_12': tbl_12, 'tbl_13': tbl_13, 'tbl_14': tbl_14, 'tbl_15': tbl_15, 'tbl_16': tbl_16, 'tbl_17': tbl_17, 'tbl_18': tbl_18, 'tbl_19': tbl_19, 'tbl_20': tbl_20, 'tbl_21': tbl_21, 'tbl_22': tbl_22, 'tbl_23': tbl_23, 'tbl_24': tbl_24, 'tbl_25': tbl_25, 'tbl_26': tbl_26, 'tbl_27': tbl_27, 'tbl_28': tbl_28, 'tbl_29': tbl_29, 'tbl_30': tbl_30, 'tbl_31': tbl_31, 'tbl_32': tbl_32, 'tbl_33': tbl_33, 'tbl_34': tbl_34, 'tbl_35': tbl_35, 'tbl_36': tbl_36, 'tbl_37': tbl_37, 'tbl_38': tbl_38, 'tbl_39': tbl_39, 'W_top1': W_top1, 'b_top1': b_top1, 'W_top2': W_top2, 'b_top2': b_top2, 'W_top3': W_top3, 'L0_rec_W': _L0_rec_in['W']}

def reference(dense_ctx, ids, tbl_0, tbl_1, tbl_2, tbl_3, tbl_4, tbl_5, tbl_6, tbl_7, tbl_8, tbl_9, tbl_10, tbl_11, tbl_12, tbl_13, tbl_14, tbl_15, tbl_16, tbl_17, tbl_18, tbl_19, tbl_20, tbl_21, tbl_22, tbl_23, tbl_24, tbl_25, tbl_26, tbl_27, tbl_28, tbl_29, tbl_30, tbl_31, tbl_32, tbl_33, tbl_34, tbl_35, tbl_36, tbl_37, tbl_38, tbl_39, W_top1, b_top1, W_top2, b_top2, W_top3, L0_rec_W):
    import jax
    import jax.numpy as jnp

    def _L0_rec_ref(x, W):
        import jax, jax.numpy as jnp
        import numpy as np

        def _pair_indices(num_fields):
            i_idx, j_idx = np.triu_indices(num_fields, k=1)
            return (jnp.asarray(i_idx), jnp.asarray(j_idx))
        B, F, D = x.shape
        i_idx, j_idx = _pair_indices(F)
        vi = x[:, i_idx, :]
        vj = x[:, j_idx, :]
        viW = jnp.einsum('bpd,pde->bpe', vi, W)
        out = jnp.einsum('bpe,bpe->bp', viW, vj)
        return out
    e = jnp.stack([tbl_0[ids[:, 0]], tbl_1[ids[:, 1]], tbl_2[ids[:, 2]], tbl_3[ids[:, 3]], tbl_4[ids[:, 4]], tbl_5[ids[:, 5]], tbl_6[ids[:, 6]], tbl_7[ids[:, 7]], tbl_8[ids[:, 8]], tbl_9[ids[:, 9]], tbl_10[ids[:, 10]], tbl_11[ids[:, 11]], tbl_12[ids[:, 12]], tbl_13[ids[:, 13]], tbl_14[ids[:, 14]], tbl_15[ids[:, 15]], tbl_16[ids[:, 16]], tbl_17[ids[:, 17]], tbl_18[ids[:, 18]], tbl_19[ids[:, 19]], tbl_20[ids[:, 20]], tbl_21[ids[:, 21]], tbl_22[ids[:, 22]], tbl_23[ids[:, 23]], tbl_24[ids[:, 24]], tbl_25[ids[:, 25]], tbl_26[ids[:, 26]], tbl_27[ids[:, 27]], tbl_28[ids[:, 28]], tbl_29[ids[:, 29]], tbl_30[ids[:, 30]], tbl_31[ids[:, 31]], tbl_32[ids[:, 32]], tbl_33[ids[:, 33]], tbl_34[ids[:, 34]], tbl_35[ids[:, 35]], tbl_36[ids[:, 36]], tbl_37[ids[:, 37]], tbl_38[ids[:, 38]], tbl_39[ids[:, 39]]], axis=1)
    z = _L0_rec_ref(e, L0_rec_W)
    z = z.reshape(z.shape[0], -1)
    h = jnp.concatenate([z, dense_ctx], axis=1)
    h = jnp.maximum(h @ W_top1 + b_top1, 0.0)
    h = jnp.maximum(h @ W_top2 + b_top2, 0.0)
    y = h @ W_top3
    return y

_drawn_inputs = setup_inputs


def setup_inputs(seed=0):
    import zlib

    import numpy as np

    out = dict(_drawn_inputs(seed))
    spreads = {'b_top1': (0.0, 0.1), 'b_top2': (0.0, 0.1)}
    factors = {}
    for name, (base, spread) in spreads.items():
        noise = np.random.default_rng([zlib.crc32(name.encode()), seed]).standard_normal(out[name].shape)
        drawn = base * np.exp(spread * noise) if base else spread * noise
        out[name] = jnp.asarray(drawn.astype(out[name].dtype))
    for name, factor in factors.items():
        out[name] = (out[name] * factor).astype(out[name].dtype)
    return out
```

```python
from contextlib import ExitStack

import numpy as np

import concourse.bass as bass
from concourse import mybir

F32 = mybir.dt.float32
F32R = mybir.dt.float32r
I32 = mybir.dt.int32
ALU = mybir.AluOpType
ACT = mybir.ActivationFunctionType

P = 128
B, F, D = 512, 40, 64
BT = B // P
NPAIR = F // 2
ND = 16
N1, N2 = 512, 256
SEL_ROWS = 32
BANK_TILES = 64
CHUNK_STEPS = 8
SLOTS = 2 * CHUNK_STEPS
RAW, HL, STAT = 3, 2, 3
UB, PB = 3, 4


def plan():
    blocks = []
    for k in reversed(range(NPAIR)):
        steps = []
        for m in reversed(range(k + 1, NPAIR)):
            if k % 2 == 0 and m == k + 1:
                steps.append([(2 * k, (2 * m, 2 * m + 1), ("pair", m)), (2 * k + 1, (2 * k, 2 * m), ("even", k // 2))])
            else:
                steps.append([(2 * k + c, (2 * m, 2 * m + 1), ("pair", m)) for c in range(2)])
        if k % 2:
            steps.append([(2 * k + 1, (2 * k - 1, 2 * k), ("odd", k // 2))])
        blocks.append((k, steps))
    return blocks


BLOCKS = plan()
STEPS = [(k, n, st) for k, steps in BLOCKS for n, st in enumerate(steps)]
TILES = [(s, c) for s, (_, _, st) in enumerate(STEPS) for c in range(len(st))]
NS, NT = len(STEPS), len(TILES)
NCHUNK = NS // CHUNK_STEPS
NBANK = -(-NT // BANK_TILES)
LAST = NT - (NBANK - 1) * BANK_TILES
assert NS % CHUNK_STEPS == 0 and NT * 2 == F * (F - 1) // 2 and LAST % 3 == 0


def z_place(n):
    bank, i = divmod(n, BANK_TILES)
    q, across = (i % 4, 4) if bank < NBANK - 1 else (i % 3, 3)
    return bank, q, i // across


def z_groups():
    groups, n = [], 0
    while n < NT:
        w = 4 if n // BANK_TILES < NBANK - 1 else 3
        groups.append(list(range(n, n + w)))
        n += w
    return groups


GROUPS = z_groups()


def build(nc, dense_t, ids, tables, w_pairs, w1_main, w1_last, w1_dense, b1, w2, b2, w3, out):
    with ExitStack() as ctx:
        def sb(name, shape, dt=F32):
            return ctx.enter_context(nc.sbuf_tensor(name, shape, dt))

        def ps(name, shape):
            return ctx.enter_context(nc.psum_tensor(name, shape, F32))

        def sem(name):
            return ctx.enter_context(nc.semaphore(name))

        idx = sb("idx", [P, BT, F], I32)
        rows = sb("rows", [P, F * BT * D])
        rows_v = rows[:, :].rearrange("p (k q c d) -> p k q c d", k=NPAIR, q=BT, c=2)
        V = sb("V", [P, NPAIR, B])
        VX = sb("VX", [P, 2, B])
        xs = sb("xs", [P, 2, 2, B], F32R)
        X = sb("X", [P, 2, 2, 2, B], F32R)
        wraw = sb("wraw", [P, RAW, SLOTS * D])
        wh = sb("wh", [P, HL, SLOTS * D], F32R)
        wl = sb("wl", [P, HL, SLOTS * D], F32R)
        wst = sb("wst", [P, STAT, SLOTS, 2 * D], F32R)
        prod = sb("prod", [P, PB, 2, B])
        zT = sb("zT", [P, NBANK, B])
        ident = sb("ident", [P, P])
        sel = sb("sel", [P, 2 * SEL_ROWS - 2])
        b1_sb = sb("b1_sb", [P, N1 // P])
        b2_sb = sb("b2_sb", [P, N2 // P])
        w3_sb = sb("w3_sb", [P, N2 // P])
        y_sb = sb("y_sb", [1, B])
        mlp_fields = (NBANK * N1 + N1 // P * N2) // (BT * D)
        mlp = rows[:, (F - mlp_fields) * BT * D:]
        w1_sb = mlp[:, 0:NBANK * N1].rearrange("p (k n) -> p k n", k=NBANK)
        w2_sb = mlp[:, NBANK * N1:].rearrange("p (k n) -> p k n", k=N1 // P)
        mlp_pair = (F - mlp_fields) // 2
        h1 = prod[:, 0:2].rearrange("p a c b -> p (a c) b")
        h2 = prod[:, 2]

        U = [ps(f"U{i}", [P, 2, B]) for i in range(UB)]
        zp = ps("zp", [P, B])
        T = ps("T", [P, B])

        ids_in = sem("ids_in")
        small_in = sem("small_in")
        w_mlp_in = sem("w_mlp_in")
        ident0, ident_ready = sem("ident0"), sem("ident_ready")
        sel0, sel_ready = sem("sel0"), sem("sel_ready")
        w1_zeroed = sem("w1_zeroed")
        rows_in = [sem(f"rows_in{k}") for k in range(NPAIR)]
        transposed = sem("transposed")
        v_saved, t_saved = sem("v_saved"), sem("t_saved")
        vx_in = sem("vx_in")
        x_low = sem("x_low")
        x_in = [sem(f"x_in{i}") for i in range(2)]
        raw_in = [sem(f"raw_in{i}") for i in range(RAW)]
        w_high, w_low = sem("w_high"), sem("w_low")
        stat_in = [sem(f"stat_in{i}") for i in range(STAT)]
        u_done = sem("u_done")
        mult_done = sem("mult_done")
        z_done = sem("z_done")
        z_saved = sem("z_saved")
        h_done, h_saved = sem("h_done"), sem("h_saved")
        y_done, y_saved, y_out = sem("y_done"), sem("y_saved"), sem("y_out")

        order = [("T", NPAIR - 1)]
        s = 0
        for k, steps in BLOCKS:
            if k:
                order.append(("T", k - 1))
            for _ in steps:
                order.append(("U", s))
                s += 1
        last_step_of = {}
        for s, (k, _, _) in enumerate(STEPS):
            last_step_of[k] = s
        first_step_of = {k: last_step_of[k] - len(steps) + 1 for k, steps in BLOCKS}
        step_of_tile = [s for s, _ in TILES]
        first_tile = {}
        for n, (s, c) in enumerate(TILES):
            first_tile.setdefault(s, n)
        group_of_tile = {n: g for g, tiles in enumerate(GROUPS) for n in tiles}
        last_group_of_bank = {n // BANK_TILES: g for g, tiles in enumerate(GROUPS) for n in tiles}
        Z_LAG = 2

        def arrival(k):
            return NPAIR - 1 - k

        block = ctx.enter_context(nc.Block())

        @block.gpsimd
        def _(pool):
            pool.memset(ident[:, :], 0.0).then_inc(ident0, 1)
            pool.wait_ge(ident0, 1)
            pool.affine_select(out=ident[:, :], in_=ident[:, :], compare_op=ALU.not_equal, fill=1.0, base=0,
                               pattern=[[-1, P]], channel_multiplier=1).then_inc(ident_ready, 1)
            pool.wait_ge(ids_in, 16)
            for k in reversed(range(NPAIR)):
                for f in (2 * k, 2 * k + 1):
                    for q in range(BT):
                        pool.indirect_dma_start(rows_v[:, k, q, f % 2, :], None, tables[f],
                                                bass.IndirectOffsetOnAxis(ap=idx[:, q, f:f + 1], axis=0)
                                                ).then_inc(rows_in[k], 16)
            pool.wait_ge(transposed, arrival(mlp_pair) + 1)
            pool.memset(w1_sb[0:96, NBANK - 1, :], 0.0).then_inc(w1_zeroed, 1)

        @block.sync
        def _(sp):
            sp.dma_start(idx[:, :, :], ids.rearrange("(q p) f -> p q f", p=P)).then_inc(ids_in, 16)

            def load_raw(j):
                if j >= RAW:
                    sp.wait_ge(w_low, j - RAW + 1)
                sp.dma_start(wraw[:, j % RAW, :], w_pairs[j]).then_inc(raw_in[j % RAW], 16)

            def spread_weights(j):
                sp.wait_ge(w_high, j + 1)
                sp.wait_ge(w_low, j + 1)
                if j >= STAT:
                    sp.wait_ge(u_done, CHUNK_STEPS * (j - STAT + 1))
                for half, part in enumerate((wh, wl)):
                    for q in range(2):
                        sp.dma_start(wst[half * D:(half + 1) * D, j % STAT, :, q * D:(q + 1) * D].bitcast(F32),
                                     part[q * D:(q + 1) * D, j % HL, :].rearrange("p (t e) -> p t e", e=D).bitcast(F32)
                                     ).then_inc(stat_in[j % STAT], 16)

            def spread_pair(k):
                a = arrival(k)
                sp.wait_ge(t_saved, a + 1)
                sp.wait_ge(x_low, a + 1)
                if a >= 2:
                    sp.wait_ge(u_done, last_step_of[k + 2] + 1)
                for c in range(2):
                    for half in range(2):
                        sp.dma_start(X[half * D:(half + 1) * D, a % 2, c].bitcast(F32),
                                     xs[c * D:(c + 1) * D, a % 2].bitcast(F32)).then_inc(x_in[a % 2], 16)

            def place_pairs(l):
                sp.wait_ge(v_saved, arrival(2 * l) + 1)
                if 2 * l + 2 < NPAIR:
                    sp.wait_ge(mult_done, last_step_of[2 * l + 2] + 1)
                for i in range(2):
                    sp.dma_start(VX[0:D, i, :], V[i * D:(i + 1) * D, 2 * l, :]).then_inc(vx_in, 16)
                    sp.dma_start(VX[D:P, i, :], V[0:D, 2 * l + 1, :]).then_inc(vx_in, 16)

            for j in range(RAW):
                load_raw(j)
            sp.dma_start(b1_sb[:, :], b1).then_inc(small_in, 16)
            sp.dma_start(b2_sb[:, :], b2).then_inc(small_in, 16)
            sp.dma_start(w3_sb[:, :], w3).then_inc(small_in, 16)
            sp.dma_start(zT[96:96 + ND, NBANK - 1, :], dense_t).then_inc(small_in, 16)
            for j in range(2):
                spread_weights(j)
            load_raw(3)
            for what, x in order:
                if what == "T":
                    spread_pair(x)
                    if x % 2 == 0:
                        place_pairs(x // 2)
                if what == "U" and x % CHUNK_STEPS == 0:
                    c = x // CHUNK_STEPS
                    if c + 2 < NCHUNK:
                        spread_weights(c + 2)
                    if c + 4 < NCHUNK:
                        load_raw(c + 4)
            sp.wait_ge(w1_zeroed, 1)
            sp.dma_start(w1_sb[:, 0:NBANK - 1, :], w1_main).then_inc(w_mlp_in, 16)
            for q in range(3):
                n = 2 * LAST // 3
                sp.dma_start(w1_sb[32 * q:32 * q + n, NBANK - 1, :], w1_last[q]).then_inc(w_mlp_in, 16)
            sp.dma_start(w1_sb[96:96 + ND, NBANK - 1, :], w1_dense).then_inc(w_mlp_in, 16)
            sp.dma_start(w2_sb, w2).then_inc(w_mlp_in, 16)
            sp.wait_ge(y_saved, 1)
            sp.dma_start(out.rearrange("b o -> o b"), y_sb[0:1, :]).then_inc(y_out, 16)
            sp.wait_ge(y_out, 16)

        @block.scalar
        def _(act):
            def split_high(j):
                act.wait_ge(raw_in[j % RAW], 16 * (j // RAW + 1))
                if j >= HL:
                    i = j - HL
                    act.wait_ge(stat_in[i % STAT], 64 * (i // STAT + 1))
                nc.scalar.copy(wh[:, j % HL, :], wraw[:, j % RAW, :]).then_inc(w_high, 1)

            def save_transposes(k):
                a = arrival(k)
                act.wait_ge(transposed, a + 1)
                nc.scalar.copy(V[:, k, :], T[:, :]).then_inc(v_saved, 1)
                if a >= 2:
                    act.wait_ge(x_in[a % 2], 64 * (a // 2))
                nc.scalar.copy(xs[:, a % 2, 0, :], T[:, :]).then_inc(t_saved, 1)

            def save_z(bank):
                act.wait_ge(z_done, last_group_of_bank[bank] + 1)
                n = P if bank < NBANK - 1 else 96
                nc.scalar.copy(zT[0:n, bank, :], zp[0:n, :]).then_inc(z_saved, 1)

            for j in range(2):
                split_high(j)
            g, saved = 0, 0
            for what, x in order:
                if what == "T":
                    save_transposes(x)
                else:
                    if x % CHUNK_STEPS == 0 and x // CHUNK_STEPS + 2 < NCHUNK:
                        split_high(x // CHUNK_STEPS + 2)
                    while g < len(GROUPS) and step_of_tile[GROUPS[g][-1]] <= x - Z_LAG:
                        g += 1
                    while saved < NBANK - 1 and last_group_of_bank[saved] < g:
                        save_z(saved)
                        saved += 1
            while saved < NBANK:
                save_z(saved)
                saved += 1
            act.wait_ge(small_in, 64)
            for n in range(N1 // P):
                act.wait_ge(h_done, n + 1)
                nc.scalar.activation(h1[:, n, :], U[n // 2][:, n % 2, :], ACT.Relu,
                                     bias=b1_sb[:, n:n + 1]).then_inc(h_saved, 1)
            for n in range(N2 // P):
                act.wait_ge(h_done, N1 // P + n + 1)
                nc.scalar.activation(h2[:, n, :], U[2][:, n, :], ACT.Relu,
                                     bias=b2_sb[:, n:n + 1]).then_inc(h_saved, 1)
            act.wait_ge(y_done, 1)
            nc.scalar.copy(y_sb[0:1, :], T[0:1, :]).then_inc(y_saved, 1)

        @block.vector
        def _(dve):
            def split_low(j):
                dve.wait_ge(w_high, j + 1)
                if j >= HL:
                    i = j - HL
                    dve.wait_ge(stat_in[i % STAT], 64 * (i // STAT + 1))
                nc.vector.tensor_tensor(wl[:, j % HL, :], wraw[:, j % RAW, :], wh[:, j % HL, :].bitcast(F32),
                                        ALU.subtract).then_inc(w_low, 1)

            def split_pair(k):
                a = arrival(k)
                dve.wait_ge(t_saved, a + 1)
                nc.vector.tensor_tensor(xs[:, a % 2, 1, :], V[:, k, :], xs[:, a % 2, 0, :].bitcast(F32),
                                        ALU.subtract).then_inc(x_low, 1)

            def multiply(s):
                k, n, st = STEPS[s]
                names = [kind for _, _, kind in st]
                dve.wait_ge(u_done, s + 1)
                if s >= PB:
                    old = s - PB
                    dve.wait_ge(z_done, group_of_tile[first_tile[old] + len(STEPS[old][2]) - 1] + 1)
                pairs = [m for name, m in names if name == "pair"]
                if pairs:
                    dve.wait_ge(v_saved, arrival(min(pairs)) + 1)
                for name, l in names:
                    if name != "pair":
                        dve.wait_ge(vx_in, 64 * (NPAIR // 2 - l))
                p, u = prod[:, s % PB], U[s % UB]
                if len(st) == 1:
                    last = nc.vector.tensor_tensor(p[:, 0, :], u[:, 0, :], VX[:, 1, :], ALU.mult)
                elif names[1][0] == "even":
                    nc.vector.tensor_tensor(p[:, 0, :], u[:, 0, :], V[:, names[0][1], :], ALU.mult)
                    last = nc.vector.tensor_tensor(p[:, 1, :], u[:, 1, :], VX[:, 0, :], ALU.mult)
                else:
                    m = names[0][1]
                    last = nc.vector.tensor_tensor(p[:, :, :], u[:, :, :],
                                                   V[:, m:m + 1, :].broadcast_to([P, 2, B]), ALU.mult)
                last.then_inc(mult_done, 1)

            nc.vector.memset(sel[:, :], 0.0).then_inc(sel0, 1)
            dve.wait_ge(sel0, 1)
            for q in range(2):
                nc.vector.memset(sel[q * D:(q + 1) * D, SEL_ROWS - 2 + q:SEL_ROWS - 1 + q], 1.0).then_inc(sel_ready, 1)
            for j in range(2):
                split_low(j)
            waiting = []
            for what, x in order:
                if what == "T":
                    waiting.append((x, 1))
                else:
                    multiply(x)
                    if x % CHUNK_STEPS == 0 and x // CHUNK_STEPS + 2 < NCHUNK:
                        split_low(x // CHUNK_STEPS + 2)
                    waiting = [(k, n - 1) for k, n in waiting]
                due = [k for k, n in waiting if n < 0 or what == "T" and (x == NPAIR - 1 or len(BLOCKS[arrival(x) - 1][1]) < 3)
                       or what == "U" and x == last_step_of[STEPS[x][0]]]
                for k in due:
                    split_pair(k)
                waiting = [(k, n) for k, n in waiting if k not in due]

        @block.tensor
        def _(pe):
            def transposes(k):
                a = arrival(k)
                if a == 0:
                    pe.wait_ge(ident_ready, 1)
                else:
                    pe.wait_ge(t_saved, a)
                pe.wait_ge(rows_in[k], 2 * BT * 16)
                for q in range(BT):
                    last = nc.tensor.transpose(T[:, q * P:(q + 1) * P],
                                               rows_v[:, k, q, :, :].rearrange("p c d -> p (c d)"), ident[:, :])
                last.then_inc(transposed, 1)

            def products(s):
                k, n, st = STEPS[s]
                a = arrival(k)
                chunk = s // CHUNK_STEPS
                if s % CHUNK_STEPS == 0:
                    pe.wait_ge(stat_in[chunk % STAT], 64 * (chunk // STAT + 1))
                if n == 0:
                    pe.wait_ge(x_in[a % 2], 64 * (a // 2 + 1))
                if s >= UB:
                    pe.wait_ge(mult_done, s - UB + 1)
                for c, (centre, _, _) in enumerate(st):
                    slot = 2 * (s % CHUNK_STEPS) + c
                    for part in range(2):
                        last = nc.tensor.matmul(U[s % UB][:, c, :], wst[:, chunk % STAT, slot, :],
                                                X[:, a % 2, centre % 2, part, :], start=part == 0, stop=part == 1)
                last.then_inc(u_done, 1)

            def sums(g):
                tiles = GROUPS[g]
                bank = tiles[0] // BANK_TILES
                pe.wait_ge(mult_done, step_of_tile[tiles[-1]] + 1)
                if g == 0:
                    pe.wait_ge(sel_ready, 2)
                if tiles[0] % BANK_TILES == 0 and bank:
                    pe.wait_ge(z_saved, bank)
                for n in tiles:
                    _, q, r = z_place(n)
                    s, c = TILES[n]
                    of_quadrant = [m for m in range(bank * BANK_TILES, min(NT, (bank + 1) * BANK_TILES))
                                   if z_place(m)[1] == q]
                    last = nc.tensor.matmul(zp[SEL_ROWS * q:SEL_ROWS * (q + 1), :],
                                            sel[:, SEL_ROWS - 2 - 2 * r:2 * SEL_ROWS - 2 - 2 * r],
                                            prod[:, s % PB, c, :], start=n == of_quadrant[0],
                                            stop=n == of_quadrant[-1])
                last.then_inc(z_done, 1)

            g = 0
            for what, x in order:
                if what == "T":
                    transposes(x)
                else:
                    products(x)
                    while g < len(GROUPS) and step_of_tile[GROUPS[g][-1]] <= x - Z_LAG:
                        sums(g)
                        g += 1
            while g < len(GROUPS):
                sums(g)
                g += 1

            pe.wait_ge(w_mlp_in, 16 * 6)
            pe.wait_ge(small_in, 64)
            pe.wait_ge(z_saved, NBANK - 1)
            pe.wait_ge(mult_done, NS)
            for n in range(N1 // P):
                for b in range(NBANK - 1):
                    nc.tensor.matmul(U[n // 2][:, n % 2, :], w1_sb[:, b, n * P:(n + 1) * P], zT[:, b, :],
                                     start=b == 0, stop=False)
            pe.wait_ge(z_saved, NBANK)
            for n in range(N1 // P):
                nc.tensor.matmul(U[n // 2][:, n % 2, :], w1_sb[0:96 + ND, NBANK - 1, n * P:(n + 1) * P],
                                 zT[0:96 + ND, NBANK - 1, :], start=False, stop=True).then_inc(h_done, 1)
            for n in range(N2 // P):
                for b in range(N1 // P):
                    if n == 0:
                        pe.wait_ge(h_saved, b + 1)
                    last = nc.tensor.matmul(U[2][:, n, :], w2_sb[:, b, n * P:(n + 1) * P], h1[:, b, :],
                                            start=b == 0, stop=b == N1 // P - 1)
                last.then_inc(h_done, 1)
            pe.wait_ge(t_saved, NPAIR)
            for b in range(N2 // P):
                pe.wait_ge(h_saved, N1 // P + b + 1)
                last = nc.tensor.matmul(T[0:1, :], w3_sb[:, b:b + 1], h2[:, b, :], start=b == 0,
                                        stop=b == N2 // P - 1)
            last.then_inc(y_done, 1)


def laid_out(inputs):
    W = np.asarray(inputs["L0_rec_W"])
    number = {pair: n for n, pair in enumerate(zip(*np.triu_indices(F, k=1)))}
    zeros = np.zeros((D, D), W.dtype)
    w = [[[zeros, zeros] for _ in range(SLOTS)] for _ in range(NCHUNK)]
    order = []
    for n, (s, c) in enumerate(TILES):
        centre, partners, _ = STEPS[s][2][c]
        for q, j in enumerate(partners):
            p = number[(min(centre, j), max(centre, j))]
            w[s // CHUNK_STEPS][2 * (s % CHUNK_STEPS) + c][q] = W[p] if centre < j else W[p].T
            order.append(p)
    w_pairs = np.array(w).transpose(0, 2, 3, 1, 4).reshape(NCHUNK, P, SLOTS * D)
    W1 = np.asarray(inputs["W_top1"])
    main = np.zeros((NBANK - 1, P), np.int64)
    last = np.zeros((3, 2 * LAST // 3), np.int64)
    for n in range(NT):
        bank, q, r = z_place(n)
        for half in range(2):
            p = order[2 * n + half]
            if bank < NBANK - 1:
                main[bank, SEL_ROWS * q + 2 * r + half] = p
            else:
                last[q, 2 * r + half] = p
    W2 = np.asarray(inputs["W_top2"])
    return {
        "dense_t": np.asarray(inputs["dense_ctx"]).T,
        "ids": np.asarray(inputs["ids"]),
        **{f"tbl_{f}": np.asarray(inputs[f"tbl_{f}"]) for f in range(F)},
        "w_pairs": w_pairs,
        "w1_main": W1[main].transpose(1, 0, 2),
        "w1_last": W1[last],
        "w1_dense": W1[F * (F - 1) // 2:],
        "b1": np.asarray(inputs["b_top1"]).reshape(N1 // P, P).T,
        "w2": W2.reshape(N1 // P, P, N2).transpose(1, 0, 2),
        "b2": np.asarray(inputs["b_top2"]).reshape(N2 // P, P).T,
        "w3": np.asarray(inputs["W_top3"]).reshape(N2 // P, P).T,
    }


def kernel(**inputs):
    import concourse.bacc as bacc
    from concourse.bass_utils import run_bass_kernel_spmd

    nc = bacc.Bacc("TRN2", target_bir_lowering=False, num_devices=1)
    arrays, aps = {}, {}
    for name, a in laid_out(inputs).items():
        a = np.ascontiguousarray(a)
        arrays[f"in_{name}"] = a
        aps[name] = nc.dram_tensor(f"in_{name}", a.shape, mybir.dt.from_np(a.dtype), kind="ExternalInput").ap()
    out = nc.dram_tensor("out_y", (B, 1), F32, kind="ExternalOutput").ap()
    tables = [aps.pop(f"tbl_{f}") for f in range(F)]
    build(nc, tables=tables, out=out, **aps)
    r = run_bass_kernel_spmd(nc, [arrays], core_ids=[0])
    return r.results[0]["out_y"]
```

```python
from contextlib import ExitStack

import numpy as np

import concourse.bass as bass
from concourse import mybir

F32 = mybir.dt.float32
F32R = mybir.dt.float32r
I32 = mybir.dt.int32
ALU = mybir.AluOpType
ACT = mybir.ActivationFunctionType

P = 128
B, F, D = 512, 40, 64
BT = B // P
NPAIR = F // 2
ND = 16
N1, N2 = 512, 256
SEL_ROWS = 32
BANK_TILES = 64
CHUNK_STEPS = 8
SLOTS = 2 * CHUNK_STEPS
RAW, HL, STAT = 3, 2, 3
XB = 3
TR = 125
PICKED = [19, 17, 15]
UNITS = 3
UB, PB = 3, 4


def plan():
    blocks = []
    for k in reversed(range(NPAIR)):
        steps = []
        for m in reversed(range(k + 1, NPAIR)):
            if k % 2 == 0 and m == k + 1:
                steps.append([(2 * k, (2 * m, 2 * m + 1), ("pair", m)), (2 * k + 1, (2 * k, 2 * m), ("even", k // 2))])
            else:
                steps.append([(2 * k + c, (2 * m, 2 * m + 1), ("pair", m)) for c in range(2)])
        if k % 2:
            steps.append([(2 * k + 1, (2 * k - 1, 2 * k), ("odd", k // 2))])
        blocks.append((k, steps))
    return blocks


BLOCKS = plan()
STEPS = [(k, n, st) for k, steps in BLOCKS for n, st in enumerate(steps)]
TILES = [(s, c) for s, (_, _, st) in enumerate(STEPS) for c in range(len(st))]
NS, NT = len(STEPS), len(TILES)
NCHUNK = NS // CHUNK_STEPS
NBANK = -(-NT // BANK_TILES)
LAST = NT - (NBANK - 1) * BANK_TILES
assert NS % CHUNK_STEPS == 0 and NT * 2 == F * (F - 1) // 2 and LAST % 3 == 0


def z_place(n):
    bank, i = divmod(n, BANK_TILES)
    q, across = (i % 4, 4) if bank < NBANK - 1 else (i % 3, 3)
    return bank, q, i // across


def z_groups():
    groups, n = [], 0
    while n < NT:
        w = 4 if n // BANK_TILES < NBANK - 1 else 3
        groups.append(list(range(n, n + w)))
        n += w
    return groups


GROUPS = z_groups()


def build(nc, dense_t, ids, ids_t, tables, w_pairs, w1_main, w1_last, w1_dense, b1, w2, b2, w3, out):
    with ExitStack() as ctx:
        def sb(name, shape, dt=F32):
            return ctx.enter_context(nc.sbuf_tensor(name, shape, dt))

        def ps(name, shape):
            return ctx.enter_context(nc.psum_tensor(name, shape, F32))

        def sem(name):
            return ctx.enter_context(nc.semaphore(name))

        idx = sb("idx", [P, BT, F], I32)
        rows = sb("rows", [P, F * BT * D])
        rows_v = rows[:, :].rearrange("p (k q c d) -> p k q c d", k=NPAIR, q=BT, c=2)
        V = sb("V", [P, NPAIR, B])
        VX = sb("VX", [P, 2, B])
        xs = sb("xs", [P, 2, 2, B], F32R)
        X = sb("X", [P, XB, 2, 2, B], F32R)
        wraw = sb("wraw", [P, RAW, SLOTS * D])
        wh = sb("wh", [P, HL, SLOTS * D], F32R)
        wl = sb("wl", [P, HL, SLOTS * D], F32R)
        wst = sb("wst", [P, STAT, SLOTS, 2 * D], F32R)
        prod = sb("prod", [P, PB, 2, B])
        zT = sb("zT", [P, NBANK, B])
        ident = sb("ident", [P, P])
        sel = sb("sel", [P, 2 * SEL_ROWS - 2])
        b1_sb = sb("b1_sb", [P, N1 // P])
        b2_sb = sb("b2_sb", [P, N2 // P])
        w3_sb = sb("w3_sb", [P, N2 // P])
        y_sb = sb("y_sb", [1, B])
        mlp_fields = (NBANK * N1 + N1 // P * N2) // (BT * D)
        mlp = rows[:, (F - mlp_fields) * BT * D:]
        w1_sb = mlp[:, 0:NBANK * N1].rearrange("p (k n) -> p k n", k=NBANK)
        w2_sb = mlp[:, NBANK * N1:].rearrange("p (k n) -> p k n", k=N1 // P)
        mlp_pair = (F - mlp_fields) // 2
        h1 = prod[:, 0:2].rearrange("p a c b -> p (a c) b")
        h2 = prod[:, 2]

        PER = {k: [tables[2 * k + c].shape[0] // TR for c in range(2)] for k in PICKED}
        RMAX = max(max(v) for v in PER.values())
        assert all(tables[2 * k + c].shape[0] == TR * PER[k][c] for k in PICKED for c in range(2))
        tab = rows[:, 0:2 * 2 * RMAX * D].rearrange("p (i c n) -> p i c n", i=2, c=2)
        idb = rows[:, 2 * 2 * RMAX * D:2 * 2 * RMAX * D + 4 * B].bitcast(I32).rearrange("p (i c b) -> p i c b", i=2, c=2)
        picked_under = -(-(4 * RMAX * D + 4 * B) // (2 * BT * D))
        one = zT[:, 0:2 * UNITS, :].rearrange("p (u c) b -> p u c b", c=2)
        row0 = sb("row0", [P, 2 * len(PICKED)])

        U = [ps(f"U{i}", [P, 2, B]) for i in range(UB)]
        zp = ps("zp", [P, B])
        T = ps("T", [P, B])

        ids_in = sem("ids_in")
        small_in = sem("small_in")
        w_mlp_in = sem("w_mlp_in")
        ident0, ident_ready = sem("ident0"), sem("ident_ready")
        sel0, sel_ready = sem("sel0"), sem("sel_ready")
        w1_zeroed = sem("w1_zeroed")
        rows_in = [sem(f"rows_in{k}") for k in range(NPAIR)]
        transposed = sem("transposed")
        v_saved, t_saved = sem("v_saved"), sem("t_saved")
        vx_in = sem("vx_in")
        x_low = sem("x_low")
        x_in = [sem(f"x_in{i}") for i in range(XB)]
        row0_ready = sem("row0_ready")
        table_in = [sem(f"table_in{i}") for i in range(2)]
        one_made, one_used = sem("one_made"), sem("one_used")
        raw_in = [sem(f"raw_in{i}") for i in range(RAW)]
        w_high, w_low = sem("w_high"), sem("w_low")
        w_placed = sem("w_placed")
        u_done = sem("u_done")
        mult_done = sem("mult_done")
        z_done = sem("z_done")
        z_saved = sem("z_saved")
        h_done, h_saved = sem("h_done"), sem("h_saved")
        y_done, y_saved, y_out = sem("y_done"), sem("y_saved"), sem("y_out")

        order = [("T", NPAIR - 1), ("T", NPAIR - 2)]
        s = 0
        for k, steps in BLOCKS:
            order.append(("B", k))
            if k >= 2:
                order.append(("T", k - 2))
            for _ in steps:
                order.append(("U", s))
                s += 1
        units_before, made_before, n_units, n_made = {}, {}, 0, 0
        for k in PICKED:
            units_before[k], made_before[k] = n_units, n_made
            n_units += max(PER[k])
            n_made += sum(PER[k])
        last_step_of = {}
        for s, (k, _, _) in enumerate(STEPS):
            last_step_of[k] = s
        first_step_of = {k: last_step_of[k] - len(steps) + 1 for k, steps in BLOCKS}
        step_of_tile = [s for s, _ in TILES]
        first_tile = {}
        for n, (s, c) in enumerate(TILES):
            first_tile.setdefault(s, n)
        group_of_tile = {n: g for g, tiles in enumerate(GROUPS) for n in tiles}
        last_group_of_bank = {n // BANK_TILES: g for g, tiles in enumerate(GROUPS) for n in tiles}
        Z_LAG = 2

        def arrival(k):
            return NPAIR - 1 - k

        block = ctx.enter_context(nc.Block())

        @block.gpsimd
        def _(pool):
            pool.memset(ident[:, :], 0.0).then_inc(ident0, 1)
            pool.wait_ge(ident0, 1)
            pool.affine_select(out=ident[:, :], in_=ident[:, :], compare_op=ALU.not_equal, fill=1.0, base=0,
                               pattern=[[-1, P]], channel_multiplier=1).then_inc(ident_ready, 1)
            for i, (k, c) in enumerate((k, c) for k in PICKED for c in range(2)):
                pool.iota(row0[0:TR, i:i + 1], [[0, 1]], base=0, channel_multiplier=PER[k][c],
                          allow_small_or_imprecise_dtypes=True).then_inc(row0_ready, 1)
            pool.wait_ge(ids_in, 16)
            for k in reversed(range(NPAIR)):
                if k in PICKED:
                    continue
                if k == picked_under - 1:
                    pool.wait_ge(one_used, n_units)
                for f in (2 * k, 2 * k + 1):
                    for q in range(BT):
                        pool.indirect_dma_start(rows_v[:, k, q, f % 2, :], None, tables[f],
                                                bass.IndirectOffsetOnAxis(ap=idx[:, q, f:f + 1], axis=0)
                                                ).then_inc(rows_in[k], 16)
            pool.wait_ge(transposed, arrival(mlp_pair) + 1)
            pool.memset(w1_sb[0:96, NBANK - 1, :], 0.0).then_inc(w1_zeroed, 1)

        @block.sync
        def _(sp):
            def load_tables(k):
                i = PICKED.index(k)
                if i >= 2:
                    sp.wait_ge(one_used, units_before[PICKED[i - 1]])
                for c in range(2):
                    sp.dma_start(tab[0:TR, i % 2, c, 0:PER[k][c] * D],
                                 tables[2 * k + c].rearrange("(p r) d -> p (r d)", p=TR)).then_inc(table_in[i % 2], 16)
                sp.dma_start(idb[0:TR, i % 2], ids_t[2 * k:2 * k + 2, :].partition_broadcast(TR)
                             ).then_inc(table_in[i % 2], 16)

            load_tables(PICKED[0])
            sp.dma_start(idx[:, :, :], ids.rearrange("(q p) f -> p q f", p=P)).then_inc(ids_in, 16)

            def load_raw(j):
                if j >= RAW:
                    sp.wait_ge(w_low, j - RAW + 1)
                    sp.wait_ge(w_placed, 4 * (j - RAW + 1))
                sp.dma_start(wraw[:, j % RAW, :], w_pairs[j]).then_inc(raw_in[j % RAW], 16)

            def spread_pair(k):
                a = arrival(k)
                sp.wait_ge(t_saved, a + 1)
                sp.wait_ge(x_low, a + 1)
                if a >= XB:
                    sp.wait_ge(u_done, last_step_of[k + XB] + 1)
                for c in range(2):
                    for half in range(2):
                        sp.dma_start(X[half * D:(half + 1) * D, a % XB, c].bitcast(F32),
                                     xs[c * D:(c + 1) * D, a % 2].bitcast(F32)).then_inc(x_in[a % XB], 16)

            def place_pairs(l):
                sp.wait_ge(v_saved, arrival(2 * l) + 1)
                if 2 * l + 2 < NPAIR:
                    sp.wait_ge(mult_done, last_step_of[2 * l + 2] + 1)
                for i in range(2):
                    sp.dma_start(VX[0:D, i, :], V[i * D:(i + 1) * D, 2 * l, :]).then_inc(vx_in, 16)
                    sp.dma_start(VX[D:P, i, :], V[0:D, 2 * l + 1, :]).then_inc(vx_in, 16)

            for j in range(RAW):
                load_raw(j)
            load_tables(PICKED[1])
            sp.dma_start(b1_sb[:, :], b1).then_inc(small_in, 16)
            sp.dma_start(b2_sb[:, :], b2).then_inc(small_in, 16)
            sp.dma_start(w3_sb[:, :], w3).then_inc(small_in, 16)
            sp.dma_start(zT[96:96 + ND, NBANK - 1, :], dense_t).then_inc(small_in, 16)
            load_raw(RAW)
            for what, x in order:
                if what == "T":
                    if x == PICKED[1]:
                        load_tables(PICKED[2])
                    spread_pair(x)
                if what == "B" and x % 2:
                    place_pairs(x // 2)
                if what == "U" and x % CHUNK_STEPS == 0 and x // CHUNK_STEPS + RAW + 1 < NCHUNK:
                    load_raw(x // CHUNK_STEPS + RAW + 1)
            sp.wait_ge(w1_zeroed, 1)
            sp.dma_start(w1_sb[:, 0:NBANK - 1, :], w1_main).then_inc(w_mlp_in, 16)
            for q in range(3):
                n = 2 * LAST // 3
                sp.dma_start(w1_sb[32 * q:32 * q + n, NBANK - 1, :], w1_last[q]).then_inc(w_mlp_in, 16)
            sp.dma_start(w1_sb[96:96 + ND, NBANK - 1, :], w1_dense).then_inc(w_mlp_in, 16)
            sp.dma_start(w2_sb, w2).then_inc(w_mlp_in, 16)
            sp.wait_ge(y_saved, 1)
            sp.dma_start(out.rearrange("b o -> o b"), y_sb[0:1, :]).then_inc(y_out, 16)
            sp.wait_ge(y_out, 16)

        @block.scalar
        def _(act):
            def split_high(j):
                act.wait_ge(raw_in[j % RAW], 16 * (j // RAW + 1))
                if j >= HL:
                    act.wait_ge(w_low, j - HL + 1)
                nc.scalar.copy(wh[:, j % HL, :], wraw[:, j % RAW, :]).then_inc(w_high, 1)

            def place(j, half, q, part):
                nc.scalar.copy(wst[half * D:(half + 1) * D, j % STAT, :, q * D:(q + 1) * D],
                               part[q * D:(q + 1) * D, :].rearrange("p (t e) -> p t e", e=D)).then_inc(w_placed, 1)

            def place_weights(j):
                if j >= STAT:
                    act.wait_ge(u_done, CHUNK_STEPS * (j - STAT + 1))
                for q in range(2):
                    place(j, q, q, wraw[:, j % RAW, :])
                act.wait_ge(w_low, j + 1)
                for q in range(2):
                    place(j, 1 - q, q, wl[:, j % HL, :].bitcast(F32))

            def save_transposes(k):
                a = arrival(k)
                act.wait_ge(transposed, a + 1)
                nc.scalar.copy(V[:, k, :], T[:, :]).then_inc(v_saved, 1)
                if a >= 2:
                    act.wait_ge(x_in[(a - 2) % XB], 64 * ((a - 2) // XB + 1))
                nc.scalar.copy(xs[:, a % 2, 0, :], T[:, :]).then_inc(t_saved, 1)

            def save_z(bank):
                act.wait_ge(z_done, last_group_of_bank[bank] + 1)
                n = P if bank < NBANK - 1 else 96
                nc.scalar.copy(zT[0:n, bank, :], zp[0:n, :]).then_inc(z_saved, 1)

            for j in range(2):
                split_high(j)
            for j in range(2):
                place_weights(j)
            g, saved = 0, 0
            for what, x in order:
                if what == "T":
                    save_transposes(x)
                elif what == "U":
                    if x % CHUNK_STEPS == 0 and x // CHUNK_STEPS + 2 < NCHUNK:
                        split_high(x // CHUNK_STEPS + 2)
                    if x % CHUNK_STEPS == 2 and x // CHUNK_STEPS + 2 < NCHUNK:
                        place_weights(x // CHUNK_STEPS + 2)
                    while g < len(GROUPS) and step_of_tile[GROUPS[g][-1]] <= x - Z_LAG:
                        g += 1
                    while saved < NBANK - 1 and last_group_of_bank[saved] < g:
                        save_z(saved)
                        saved += 1
            while saved < NBANK:
                save_z(saved)
                saved += 1
            act.wait_ge(small_in, 64)
            for n in range(N1 // P):
                act.wait_ge(h_done, n + 1)
                nc.scalar.activation(h1[:, n, :], U[n // 2][:, n % 2, :], ACT.Relu,
                                     bias=b1_sb[:, n:n + 1]).then_inc(h_saved, 1)
            for n in range(N2 // P):
                act.wait_ge(h_done, N1 // P + n + 1)
                nc.scalar.activation(h2[:, n, :], U[2][:, n, :], ACT.Relu,
                                     bias=b2_sb[:, n:n + 1]).then_inc(h_saved, 1)
            act.wait_ge(y_done, 1)
            nc.scalar.copy(y_sb[0:1, :], T[0:1, :]).then_inc(y_saved, 1)

        @block.vector
        def _(dve):
            def split_low(j):
                dve.wait_ge(w_high, j + 1)
                if j >= HL:
                    dve.wait_ge(w_placed, 4 * (j - HL + 1))
                nc.vector.tensor_tensor(wl[:, j % HL, :], wraw[:, j % RAW, :], wh[:, j % HL, :].bitcast(F32),
                                        ALU.subtract).then_inc(w_low, 1)

            def split_pair(k):
                a = arrival(k)
                dve.wait_ge(t_saved, a + 1)
                nc.vector.tensor_tensor(xs[:, a % 2, 1, :], V[:, k, :], xs[:, a % 2, 0, :].bitcast(F32),
                                        ALU.subtract).then_inc(x_low, 1)

            def multiply(s):
                k, n, st = STEPS[s]
                names = [kind for _, _, kind in st]
                dve.wait_ge(u_done, s + 1)
                if s >= PB:
                    old = s - PB
                    dve.wait_ge(z_done, group_of_tile[first_tile[old] + len(STEPS[old][2]) - 1] + 1)
                pairs = [m for name, m in names if name == "pair"]
                if pairs:
                    dve.wait_ge(v_saved, arrival(min(pairs)) + 1)
                for name, l in names:
                    if name != "pair":
                        dve.wait_ge(vx_in, 64 * (NPAIR // 2 - l))
                p, u = prod[:, s % PB], U[s % UB]
                if len(st) == 1:
                    last = nc.vector.tensor_tensor(p[:, 0, :], u[:, 0, :], VX[:, 1, :], ALU.mult)
                elif names[1][0] == "even":
                    nc.vector.tensor_tensor(p[:, 0, :], u[:, 0, :], V[:, names[0][1], :], ALU.mult)
                    last = nc.vector.tensor_tensor(p[:, 1, :], u[:, 1, :], VX[:, 0, :], ALU.mult)
                else:
                    m = names[0][1]
                    last = nc.vector.tensor_tensor(p[:, :, :], u[:, :, :],
                                                   V[:, m:m + 1, :].broadcast_to([P, 2, B]), ALU.mult)
                last.then_inc(mult_done, 1)

            nc.vector.memset(sel[:, :], 0.0).then_inc(sel0, 1)
            dve.wait_ge(sel0, 1)
            for q in range(2):
                nc.vector.memset(sel[q * D:(q + 1) * D, SEL_ROWS - 2 + q:SEL_ROWS - 1 + q], 1.0).then_inc(sel_ready, 1)
            def select(k):
                i = PICKED.index(k)
                dve.wait_ge(table_in[i % 2], 48 * (i // 2 + 1))
                if i == 0:
                    dve.wait_ge(row0_ready, 2 * len(PICKED))
                for t in range(max(PER[k])):
                    unit = units_before[k] + t
                    if unit >= UNITS:
                        dve.wait_ge(one_used, unit - UNITS + 1)
                    for c in range(2):
                        if t < PER[k][c]:
                            nc.vector.tensor_scalar(one[0:TR, unit % UNITS, c, :], idb[0:TR, i % 2, c, :],
                                                    row0[0:TR, 2 * i + c:2 * i + c + 1], float(t),
                                                    ALU.subtract, ALU.is_equal).then_inc(one_made, 1)

            waiting = []
            for what, x in order:
                if what == "T":
                    if x in PICKED:
                        select(x)
                    if x == PICKED[0]:
                        for j in range(2):
                            split_low(j)
                    waiting.append((x, 1))
                elif what == "U":
                    multiply(x)
                    if x % CHUNK_STEPS == 0 and x // CHUNK_STEPS + 2 < NCHUNK:
                        split_low(x // CHUNK_STEPS + 2)
                    waiting = [(k, n - 1) for k, n in waiting]
                due = [k for k, n in waiting if n < 0 or k >= NPAIR - 2
                       or what == "U" and x == last_step_of[STEPS[x][0]]]
                for k in due:
                    split_pair(k)
                waiting = [(k, n) for k, n in waiting if k not in due]

        @block.tensor
        def _(pe):
            def transposes(k):
                a = arrival(k)
                if a:
                    pe.wait_ge(t_saved, a)
                if k in PICKED:
                    for t in range(max(PER[k])):
                        unit = units_before[k] + t
                        pe.wait_ge(one_made, made_before[k] + sum(min(t + 1, r) for r in PER[k]))
                        for c in range(2):
                            if t < PER[k][c]:
                                last = nc.tensor.matmul(T[c * D:(c + 1) * D, :],
                                                        tab[0:TR, PICKED.index(k) % 2, c, t * D:(t + 1) * D],
                                                        one[0:TR, unit % UNITS, c, :],
                                                        start=t == 0, stop=t == PER[k][c] - 1)
                        last.then_inc(one_used, 1)
                        if t == max(PER[k]) - 1:
                            pe.wait_ge(one_used, unit + 1)
                            nc.tensor.nop().then_inc(transposed, 1)
                    return
                if a == 1:
                    pe.wait_ge(ident_ready, 1)
                pe.wait_ge(rows_in[k], 2 * BT * 16)
                for q in range(BT):
                    last = nc.tensor.transpose(T[:, q * P:(q + 1) * P],
                                               rows_v[:, k, q, :, :].rearrange("p c d -> p (c d)"), ident[:, :])
                last.then_inc(transposed, 1)

            def products(s):
                k, n, st = STEPS[s]
                a = arrival(k)
                chunk = s // CHUNK_STEPS
                if s % CHUNK_STEPS == 0:
                    pe.wait_ge(w_placed, 4 * (chunk + 1))
                if n == 0:
                    pe.wait_ge(x_in[a % XB], 64 * (a // XB + 1))
                if s >= UB:
                    pe.wait_ge(mult_done, s - UB + 1)
                for c, (centre, _, _) in enumerate(st):
                    slot = 2 * (s % CHUNK_STEPS) + c
                    for part in range(2):
                        last = nc.tensor.matmul(U[s % UB][:, c, :], wst[:, chunk % STAT, slot, :],
                                                X[:, a % XB, centre % 2, part, :], start=part == 0, stop=part == 1)
                last.then_inc(u_done, 1)

            def sums(g):
                tiles = GROUPS[g]
                bank = tiles[0] // BANK_TILES
                pe.wait_ge(mult_done, step_of_tile[tiles[-1]] + 1)
                if g == 0:
                    pe.wait_ge(sel_ready, 2)
                if tiles[0] % BANK_TILES == 0 and bank:
                    pe.wait_ge(z_saved, bank)
                for n in tiles:
                    _, q, r = z_place(n)
                    s, c = TILES[n]
                    of_quadrant = [m for m in range(bank * BANK_TILES, min(NT, (bank + 1) * BANK_TILES))
                                   if z_place(m)[1] == q]
                    last = nc.tensor.matmul(zp[SEL_ROWS * q:SEL_ROWS * (q + 1), :],
                                            sel[:, SEL_ROWS - 2 - 2 * r:2 * SEL_ROWS - 2 - 2 * r],
                                            prod[:, s % PB, c, :], start=n == of_quadrant[0],
                                            stop=n == of_quadrant[-1])
                last.then_inc(z_done, 1)

            g = 0
            for what, x in order:
                if what == "T":
                    transposes(x)
                elif what == "U":
                    products(x)
                    while g < len(GROUPS) and step_of_tile[GROUPS[g][-1]] <= x - Z_LAG:
                        sums(g)
                        g += 1
            while g < len(GROUPS):
                sums(g)
                g += 1

            pe.wait_ge(w_mlp_in, 16 * 6)
            pe.wait_ge(small_in, 64)
            pe.wait_ge(z_saved, NBANK - 1)
            pe.wait_ge(mult_done, NS)
            for n in range(N1 // P):
                for b in range(NBANK - 1):
                    nc.tensor.matmul(U[n // 2][:, n % 2, :], w1_sb[:, b, n * P:(n + 1) * P], zT[:, b, :],
                                     start=b == 0, stop=False)
            pe.wait_ge(z_saved, NBANK)
            for n in range(N1 // P):
                nc.tensor.matmul(U[n // 2][:, n % 2, :], w1_sb[0:96 + ND, NBANK - 1, n * P:(n + 1) * P],
                                 zT[0:96 + ND, NBANK - 1, :], start=False, stop=True).then_inc(h_done, 1)
            for n in range(N2 // P):
                for b in range(N1 // P):
                    if n == 0:
                        pe.wait_ge(h_saved, b + 1)
                    last = nc.tensor.matmul(U[2][:, n, :], w2_sb[:, b, n * P:(n + 1) * P], h1[:, b, :],
                                            start=b == 0, stop=b == N1 // P - 1)
                last.then_inc(h_done, 1)
            pe.wait_ge(t_saved, NPAIR)
            for b in range(N2 // P):
                pe.wait_ge(h_saved, N1 // P + b + 1)
                last = nc.tensor.matmul(T[0:1, :], w3_sb[:, b:b + 1], h2[:, b, :], start=b == 0,
                                        stop=b == N2 // P - 1)
            last.then_inc(y_done, 1)


def laid_out(inputs):
    W = np.asarray(inputs["L0_rec_W"])
    number = {pair: n for n, pair in enumerate(zip(*np.triu_indices(F, k=1)))}
    zeros = np.zeros((D, D), W.dtype)
    w = [[[zeros, zeros] for _ in range(SLOTS)] for _ in range(NCHUNK)]
    order = []
    for n, (s, c) in enumerate(TILES):
        centre, partners, _ = STEPS[s][2][c]
        for q, j in enumerate(partners):
            p = number[(min(centre, j), max(centre, j))]
            w[s // CHUNK_STEPS][2 * (s % CHUNK_STEPS) + c][q] = W[p] if centre < j else W[p].T
            order.append(p)
    w_pairs = np.array(w).transpose(0, 2, 3, 1, 4).reshape(NCHUNK, P, SLOTS * D)
    W1 = np.asarray(inputs["W_top1"])
    main = np.zeros((NBANK - 1, P), np.int64)
    last = np.zeros((3, 2 * LAST // 3), np.int64)
    for n in range(NT):
        bank, q, r = z_place(n)
        for half in range(2):
            p = order[2 * n + half]
            if bank < NBANK - 1:
                main[bank, SEL_ROWS * q + 2 * r + half] = p
            else:
                last[q, 2 * r + half] = p
    W2 = np.asarray(inputs["W_top2"])
    return {
        "dense_t": np.asarray(inputs["dense_ctx"]).T,
        "ids": np.asarray(inputs["ids"]),
        "ids_t": np.asarray(inputs["ids"]).T,
        **{f"tbl_{f}": np.asarray(inputs[f"tbl_{f}"]) for f in range(F)},
        "w_pairs": w_pairs,
        "w1_main": W1[main].transpose(1, 0, 2),
        "w1_last": W1[last],
        "w1_dense": W1[F * (F - 1) // 2:],
        "b1": np.asarray(inputs["b_top1"]).reshape(N1 // P, P).T,
        "w2": W2.reshape(N1 // P, P, N2).transpose(1, 0, 2),
        "b2": np.asarray(inputs["b_top2"]).reshape(N2 // P, P).T,
        "w3": np.asarray(inputs["W_top3"]).reshape(N2 // P, P).T,
    }


def kernel(**inputs):
    import concourse.bacc as bacc
    from concourse.bass_utils import run_bass_kernel_spmd

    nc = bacc.Bacc("TRN2", target_bir_lowering=False, num_devices=1)
    arrays, aps = {}, {}
    for name, a in laid_out(inputs).items():
        a = np.ascontiguousarray(a)
        arrays[f"in_{name}"] = a
        aps[name] = nc.dram_tensor(f"in_{name}", a.shape, mybir.dt.from_np(a.dtype), kind="ExternalInput").ap()
    out = nc.dram_tensor("out_y", (B, 1), F32, kind="ExternalOutput").ap()
    tables = [aps.pop(f"tbl_{f}") for f in range(F)]
    build(nc, tables=tables, out=out, **aps)
    r = run_bass_kernel_spmd(nc, [arrays], core_ids=[0])
    return r.results[0]["out_y"]
```

```python
from contextlib import ExitStack

import numpy as np

import concourse.bass as bass
from concourse import mybir

F32 = mybir.dt.float32
F32R = mybir.dt.float32r
I32 = mybir.dt.int32
ALU = mybir.AluOpType
ACT = mybir.ActivationFunctionType

P = 128
B, F, D = 512, 40, 64
BT = B // P
NPAIR = F // 2
ND = 16
N1, N2 = 512, 256
SEL_ROWS = 32
BANK_TILES = 64
CHUNK_STEPS = 8
SLOTS = 2 * CHUNK_STEPS
RAW, HL, STAT = 3, 2, 3
XB = 3
TR = 125
PICKED = [19, 17, 15]
UNITS = 3
UB, PB = 3, 4
ROW_GROUPS = 8
ROW_SETS = [(12, 14, 16, 18), (8, 9, 10, 11)]
ROW_FIRST_BLOCK = 7
W1_ROWS = 4
ROW_SPACING = 4
PLACE_AT_ONCE = 1
ROW_SLACK = 1
POOL_FROM, POOL_TAKES, POOL_EVERY = 72, 1, 2


class Step:

    def __init__(self, k, tiles):
        self.k, self.tiles = k, tiles
        self.group = self.i = self.w = self.pairs = None
        self.on_pool = False


def plan():
    weights, groups, earliest = [], 0, 0
    for k in reversed(range(NPAIR)):
        def pair_step(m):
            return Step(k, [(2 * k + c, (2 * m, 2 * m + 1), ("pair", m)) for c in range(2)])

        ms = [m for m in reversed(range(k + 1, NPAIR)) if k % 2 or m != k + 1]
        sets = [s for s in ROW_SETS if k <= ROW_FIRST_BLOCK and s[0] > k]
        while ms:
            n = len(weights)
            if sets and groups < ROW_GROUPS and n % CHUNK_STEPS <= ROW_SLACK and n >= earliest:
                for i, m in enumerate(sets.pop(0)):
                    ms.remove(m)
                    weights.append(pair_step(m))
                    weights[-1].group, weights[-1].i = groups, i
                for st in weights[n:]:
                    st.pairs = [s.tiles[0][2][1] for s in weights[n:]]
                groups, earliest = groups + 1, n + 4 * ROW_SPACING - 1
            else:
                kept = [m for s in sets for m in s] if groups < ROW_GROUPS else []
                m = next((m for m in ms if m not in kept), ms[0])
                sets = [s for s in sets if m not in s]
                ms.remove(m)
                weights.append(pair_step(m))
        if k % 2:
            weights.append(Step(k, [(2 * k + 1, (2 * k - 1, 2 * k), ("odd", k // 2))]))
        else:
            m = k + 1
            weights.append(Step(k, [(2 * k, (2 * m, 2 * m + 1), ("pair", m)),
                                    (2 * k + 1, (2 * k, 2 * m), ("even", k // 2))]))
    assert groups == ROW_GROUPS
    steps, rows, since = [], [], ROW_SPACING
    for w, st in enumerate(weights):
        st.w = w
        if st.group is not None:
            rows.append(st)
        else:
            steps.append(st)
            since += 1
        if rows and since >= ROW_SPACING:
            steps.append(rows.pop(0))
            since = 1
    steps += rows
    n = 0
    for s, st in enumerate(steps):
        if st.group is None and s >= POOL_FROM and all(kind[0] == "pair" for _, _, kind in st.tiles):
            st.on_pool = n % POOL_EVERY < POOL_TAKES
            n += 1
    return weights, steps


WEIGHTS, STEPS = plan()
NS = len(STEPS)
TILES = [(s, c) for s, st in enumerate(STEPS) if st.group is None for c in range(len(st.tiles))]
NT = len(TILES)
NCHUNK = NS // CHUNK_STEPS
NROWBANK = ROW_GROUPS * 16 // P
NBANK = -(-NT // BANK_TILES)
NZ = NBANK + NROWBANK
LAST = NT - (NBANK - 1) * BANK_TILES
assert NS % CHUNK_STEPS == 0 and ROW_GROUPS * 16 % P == 0 and LAST % 3 == 0
assert NT * 2 + ROW_GROUPS * 16 == F * (F - 1) // 2


def z_index(bank):
    return bank if bank < NBANK - 1 else NZ - 1


def z_place(n):
    bank, i = divmod(n, BANK_TILES)
    q, across = (i % 4, 4) if bank < NBANK - 1 else (i % 3, 3)
    return bank, q, i // across


def z_groups():
    groups, n = [], 0
    while n < NT:
        w = 4 if n // BANK_TILES < NBANK - 1 else 3
        groups.append(list(range(n, n + w)))
        n += w
    return groups


GROUPS = z_groups()


def build(nc, dense_t, ids, ids_t, tables, w_pairs, w1_main, w1_last, w1_dense, b1, w2, b2, w3, out):
    with ExitStack() as ctx:
        def sb(name, shape, dt=F32):
            return ctx.enter_context(nc.sbuf_tensor(name, shape, dt))

        def ps(name, shape):
            return ctx.enter_context(nc.psum_tensor(name, shape, F32))

        def sem(name):
            return ctx.enter_context(nc.semaphore(name))

        idx = sb("idx", [P, BT, F], I32)
        rows = sb("rows", [P, F * BT * D])
        rows_v = rows[:, :].rearrange("p (k q c d) -> p k q c d", k=NPAIR, q=BT, c=2)
        V = sb("V", [P, NPAIR, B])
        VX = sb("VX", [P, 2, B])
        xs = sb("xs", [P, 2, 2, B], F32R)
        X = sb("X", [P, XB, 2, 2, B], F32R)
        wraw = sb("wraw", [P, RAW, SLOTS * D])
        wh = sb("wh", [P, HL, SLOTS * D], F32R)
        wl = sb("wl", [P, HL, SLOTS * D], F32R)
        wst = sb("wst", [P, STAT, SLOTS, 2 * D], F32R)
        prod = sb("prod", [P, PB, 2, B])
        row_prod = sb("row_prod", [P, 2, B])
        zT = sb("zT", [P, NZ, B])
        zb = zT[:, NBANK - 1:NBANK - 1 + NROWBANK].rearrange("p n (q z) -> p n q z", q=BT)
        ident = sb("ident", [P, P])
        sel = sb("sel", [P, 2 * SEL_ROWS - 2])
        b1_sb = sb("b1_sb", [P, N1 // P])
        b2_sb = sb("b2_sb", [P, N2 // P])
        w3_sb = sb("w3_sb", [P, N2 // P])
        y_sb = sb("y_sb", [1, B])
        w1_end = sb("w1_end", [P, N1])
        w1_rows = rows[:, 0:W1_ROWS * N1].rearrange("p (k n) -> p k n", k=W1_ROWS)
        w1_raw = wraw[:, (NCHUNK + 1) % RAW, :].rearrange("p (k n) -> p k n", k=2)
        w1_sb = [w1_rows[:, b, :] for b in range(W1_ROWS)] + [w1_raw[:, b, :] for b in range(2)] + [w1_end]
        w2_sb = wraw[:, NCHUNK % RAW, :].rearrange("p (k n) -> p k n", k=N1 // P)
        assert len(w1_sb) == NZ and W1_ROWS * N1 <= 4 * 2 * BT * D and N1 // P * N2 == SLOTS * D == 2 * N1
        rows_k = rows[:, :].rearrange("p (k n) -> p k n", k=NPAIR)
        dve_prod = [prod[:, i] for i in range(PB)] + [rows_k[:, 17:NPAIR:2, :]]
        pool_prod = [rows_k[:, 13:16:2, :], rows_k[:, 6:8, :], rows_k[:, 4:6, :]]
        before_5 = zT[:, NBANK - 3:NBANK - 1, :]
        POOL_ROWS = 6
        assert not {4, 5, 6, 7, 13} & {m for s in ROW_SETS for m in s} and {15, 17, 19} == set(PICKED)
        h1 = prod[:, 0:2].rearrange("p a c b -> p (a c) b")
        h2 = prod[:, 2]

        PER = {k: [tables[2 * k + c].shape[0] // TR for c in range(2)] for k in PICKED}
        RMAX = max(max(v) for v in PER.values())
        assert all(tables[2 * k + c].shape[0] == TR * PER[k][c] for k in PICKED for c in range(2))
        tab = rows[:, 0:2 * 2 * RMAX * D].rearrange("p (i c n) -> p i c n", i=2, c=2)
        idb = rows[:, 2 * 2 * RMAX * D:2 * 2 * RMAX * D + 4 * B].bitcast(I32).rearrange("p (i c b) -> p i c b", i=2, c=2)
        picked_under = -(-(4 * RMAX * D + 4 * B) // (2 * BT * D))
        one = zT[:, 0:2 * UNITS, :].rearrange("p (u c) b -> p u c b", c=2)
        row0 = sb("row0", [P, 2 * len(PICKED)])

        U = [ps(f"U{i}", [P, 2, B]) for i in range(UB)]
        zp = ps("zp", [P, B])
        T = ps("T", [P, B])

        ids_in = sem("ids_in")
        small_in = sem("small_in")
        w_mlp_in = sem("w_mlp_in")
        ident0, ident_ready = sem("ident0"), sem("ident_ready")
        sel0, sel_ready = sem("sel0"), sem("sel_ready")
        w1_zeroed = sem("w1_zeroed")
        rows_in = [sem(f"rows_in{k}") for k in range(NPAIR)]
        transposed = sem("transposed")
        v_saved, t_saved = sem("v_saved"), sem("t_saved")
        vx_in = sem("vx_in")
        x_low = sem("x_low")
        x_in = [sem(f"x_in{i}") for i in range(XB)]
        row0_ready = sem("row0_ready")
        table_in = [sem(f"table_in{i}") for i in range(2)]
        one_made, one_used = sem("one_made"), sem("one_used")
        raw_in = [sem(f"raw_in{i}") for i in range(RAW)]
        w_high, w_low, pool_w_low = sem("w_high"), sem("w_low"), sem("pool_w_low")
        w_placed = sem("w_placed")
        u_done = sem("u_done")
        mult_done = sem("mult_done")
        u_copied, pool_done = sem("u_copied"), sem("pool_done")
        row_mult, row_summed = sem("row_mult"), sem("row_summed")
        r_transposed, r_saved = sem("r_transposed"), sem("r_saved")
        z_done = sem("z_done")
        z_saved = sem("z_saved")
        h_done, h_saved = sem("h_done"), sem("h_saved")
        y_done, y_saved, y_out = sem("y_done"), sem("y_saved"), sem("y_out")

        last_step_of = {st.k: s for s, st in enumerate(STEPS)}
        first_step_of = {st.k: s for s, st in reversed(list(enumerate(STEPS)))}
        sum_steps = [s for s, st in enumerate(STEPS) if st.group is None]
        row_steps = [s for s, st in enumerate(STEPS) if st.group is not None]
        pool_steps = [s for s, st in enumerate(STEPS) if st.on_pool]
        dve_steps = [s for s in sum_steps if not STEPS[s].on_pool]
        row_number = {s: i for i, s in enumerate(row_steps)}
        pool_number = {s: i for i, s in enumerate(pool_steps)}
        dve_number = {s: i for i, s in enumerate(dve_steps)}
        last_step_of_chunk = {}
        for s, st in enumerate(STEPS):
            j = st.w // CHUNK_STEPS
            last_step_of_chunk[j] = max(s, last_step_of_chunk.get(j, 0))
        place_after = {max(CHUNK_STEPS * (j - 2) + 2, last_step_of_chunk.get(j - STAT, -1) + 1): j
                       for j in range(2, NCHUNK)}
        R_AT = 8
        order = [("T", NPAIR - 1), ("T", NPAIR - 2)]
        for s, st in enumerate(STEPS):
            if s == first_step_of[st.k]:
                order.append(("B", st.k))
                if st.k >= 2:
                    order.append(("T", st.k - 2))
            order.append(("U", s))
            for bank in range(NROWBANK):
                if s == min(NS - 1, row_steps[len(row_steps) // NROWBANK * (bank + 1) - 1] + R_AT):
                    order.append(("R", bank))
        units_before, made_before, n_units, n_made = {}, {}, 0, 0
        for k in PICKED:
            units_before[k], made_before[k] = n_units, n_made
            n_units += max(PER[k])
            n_made += sum(PER[k])
        step_of_tile = [s for s, _ in TILES]
        last_tile = {}
        for n, (s, c) in enumerate(TILES):
            last_tile[s] = n
        group_of_tile = {n: g for g, tiles in enumerate(GROUPS) for n in tiles}
        last_group_of_bank = {n // BANK_TILES: g for g, tiles in enumerate(GROUPS) for n in tiles}
        Z_LAG, POOL_LAG = 3, 5

        def summed_by(x):
            g = 0

            def due(s):
                if STEPS[s].on_pool:
                    return s + POOL_LAG <= x or pool_number[s] + len(pool_prod) <= sum(n <= x for n in pool_steps)
                return s + Z_LAG <= x or dve_number[s] + len(dve_prod) <= sum(n <= x for n in dve_steps)

            while g < len(GROUPS) and all(due(step_of_tile[n]) for n in GROUPS[g]):
                g += 1
            return g

        def wait_u_read(engine, s):
            if s in row_number:
                engine.wait_ge(row_mult, 2 * (row_number[s] + 1))
            elif s in pool_number:
                engine.wait_ge(u_copied, pool_number[s] + 1)
            else:
                engine.wait_ge(mult_done, dve_number[s] + 1)

        pool_chunks = range(POOL_FROM // CHUNK_STEPS + 3, NCHUNK)

        dve_chunks = [j for j in range(NCHUNK) if j not in pool_chunks]

        def wait_w_low(engine, j):
            if j in pool_chunks:
                engine.wait_ge(pool_w_low, pool_chunks.index(j) + 1)
            else:
                engine.wait_ge(w_low, j + 1 - sum(i <= j for i in pool_chunks))

        def wait_low_placed(engine, j):
            if j >= HL:
                engine.wait_ge(w_placed, 4 * (j - HL + 1))

        def product_buffer(s):
            if s in pool_number:
                i = pool_number[s] % len(pool_prod)
                return before_5 if i == 2 and s < first_step_of[5] else pool_prod[i]
            return dve_prod[dve_number[s] % len(dve_prod)]

        def wait_summed(engine, s):
            if s in pool_number:
                n, steps = pool_number[s] - len(pool_prod), pool_steps
            else:
                n, steps = dve_number[s] - len(dve_prod), dve_steps
            if n >= 0:
                engine.wait_ge(z_done, group_of_tile[last_tile[steps[n]]] + 1)

        def arrival(k):
            return NPAIR - 1 - k

        block = ctx.enter_context(nc.Block())

        @block.gpsimd
        def _(pool):
            def multiply(s):
                i, m = pool_number[s], STEPS[s].tiles[0][2][1]
                pool.wait_ge(u_copied, i + 1)
                pool.tensor_tensor(product_buffer(s), product_buffer(s),
                                   V[:, m:m + 1, :].broadcast_to([P, 2, B]), ALU.mult).then_inc(pool_done, 1)

            def split_low(j):
                pool.wait_ge(w_high, j + 1)
                wait_low_placed(pool, j)
                pool.tensor_tensor(wl[:, j % HL, :], wraw[:, j % RAW, :], wh[:, j % HL, :].bitcast(F32),
                                   ALU.subtract).then_inc(pool_w_low, 1)

            pool.memset(ident[:, :], 0.0).then_inc(ident0, 1)
            pool.wait_ge(ident0, 1)
            pool.affine_select(out=ident[:, :], in_=ident[:, :], compare_op=ALU.not_equal, fill=1.0, base=0,
                               pattern=[[-1, P]], channel_multiplier=1).then_inc(ident_ready, 1)
            for i, (k, c) in enumerate((k, c) for k in PICKED for c in range(2)):
                pool.iota(row0[0:TR, i:i + 1], [[0, 1]], base=0, channel_multiplier=PER[k][c],
                          allow_small_or_imprecise_dtypes=True).then_inc(row0_ready, 1)
            pool.wait_ge(ids_in, 16)
            for k in reversed(range(NPAIR)):
                if k in PICKED:
                    continue
                if k == picked_under - 1:
                    pool.wait_ge(one_used, n_units)
                for f in (2 * k, 2 * k + 1):
                    for q in range(BT):
                        pool.indirect_dma_start(rows_v[:, k, q, f % 2, :], None, tables[f],
                                                bass.IndirectOffsetOnAxis(ap=idx[:, q, f:f + 1], axis=0)
                                                ).then_inc(rows_in[k], 16)
            pool.memset(w1_end[0:96, :], 0.0).then_inc(w1_zeroed, 1)
            for s in range(POOL_FROM, NS):
                if s in pool_number:
                    multiply(s)
                if s % CHUNK_STEPS == 0 and s // CHUNK_STEPS + 2 in pool_chunks:
                    split_low(s // CHUNK_STEPS + 2)

        @block.sync
        def _(sp):
            def load_tables(k):
                i = PICKED.index(k)
                if i >= 2:
                    sp.wait_ge(one_used, units_before[PICKED[i - 1]])
                for c in range(2):
                    sp.dma_start(tab[0:TR, i % 2, c, 0:PER[k][c] * D],
                                 tables[2 * k + c].rearrange("(p r) d -> p (r d)", p=TR)).then_inc(table_in[i % 2], 16)
                sp.dma_start(idb[0:TR, i % 2], ids_t[2 * k:2 * k + 2, :].partition_broadcast(TR)
                             ).then_inc(table_in[i % 2], 16)

            load_tables(PICKED[0])
            sp.dma_start(idx[:, :, :], ids.rearrange("(q p) f -> p q f", p=P)).then_inc(ids_in, 16)

            def load_raw(j):
                if j >= RAW:
                    wait_w_low(sp, j - RAW)
                    sp.wait_ge(w_placed, 4 * (j - RAW + 1))
                sp.dma_start(wraw[:, j % RAW, :], w_pairs[j]).then_inc(raw_in[j % RAW], 16)

            def spread_pair(k):
                a = arrival(k)
                sp.wait_ge(t_saved, a + 1)
                sp.wait_ge(x_low, a + 1)
                if a >= XB:
                    sp.wait_ge(u_done, last_step_of[k + XB] + 1)
                for c in range(2):
                    for half in range(2):
                        sp.dma_start(X[half * D:(half + 1) * D, a % XB, c].bitcast(F32),
                                     xs[c * D:(c + 1) * D, a % 2].bitcast(F32)).then_inc(x_in[a % XB], 16)

            def place_pairs(l):
                sp.wait_ge(v_saved, arrival(2 * l) + 1)
                if 2 * l + 2 < NPAIR:
                    even = next(s for s in dve_steps if STEPS[s].tiles[-1][2] == ("even", l + 1))
                    sp.wait_ge(mult_done, dve_number[even] + 1)
                for i in range(2):
                    sp.dma_start(VX[0:D, i, :], V[i * D:(i + 1) * D, 2 * l, :]).then_inc(vx_in, 16)
                    sp.dma_start(VX[D:P, i, :], V[0:D, 2 * l + 1, :]).then_inc(vx_in, 16)

            for j in range(2):
                load_raw(j)
            load_tables(PICKED[1])
            for j in range(2, RAW):
                load_raw(j)
            sp.dma_start(b1_sb[:, :], b1).then_inc(small_in, 16)
            sp.dma_start(b2_sb[:, :], b2).then_inc(small_in, 16)
            sp.dma_start(w3_sb[:, :], w3).then_inc(small_in, 16)
            sp.dma_start(zT[96:96 + ND, NZ - 1, :], dense_t).then_inc(small_in, 16)
            load_raw(RAW)
            for what, x in order:
                if what == "T":
                    if x == NPAIR - 2:
                        load_tables(PICKED[2])
                    spread_pair(x)
                if what == "B" and x % 2:
                    place_pairs(x // 2)
                if what == "U" and x % CHUNK_STEPS == 0 and x // CHUNK_STEPS + RAW + 1 < NCHUNK:
                    load_raw(x // CHUNK_STEPS + RAW + 1)
            sp.wait_ge(w1_zeroed, 1)
            sp.wait_ge(transposed, NPAIR)
            sp.dma_start(w1_rows, w1_main[:, 0:W1_ROWS]).then_inc(w_mlp_in, 16)
            for q in range(3):
                n = 2 * LAST // 3
                sp.dma_start(w1_end[32 * q:32 * q + n, :], w1_last[q]).then_inc(w_mlp_in, 16)
            sp.dma_start(w1_end[96:96 + ND, :], w1_dense).then_inc(w_mlp_in, 16)
            wait_w_low(sp, NCHUNK - RAW)
            sp.wait_ge(w_placed, 4 * (NCHUNK - RAW + 1))
            sp.dma_start(w2_sb, w2).then_inc(w_mlp_in, 16)
            wait_w_low(sp, NCHUNK - RAW + 1)
            sp.wait_ge(w_placed, 4 * (NCHUNK - RAW + 2))
            sp.dma_start(w1_raw, w1_main[:, W1_ROWS:]).then_inc(w_mlp_in, 16)
            sp.wait_ge(y_saved, 1)
            sp.dma_start(out.rearrange("b o -> o b"), y_sb[0:1, :]).then_inc(y_out, 16)
            sp.wait_ge(y_out, 16)

        @block.scalar
        def _(act):
            def split_high(j):
                act.wait_ge(raw_in[j % RAW], 16 * (j // RAW + 1))
                if j >= HL:
                    wait_w_low(act, j - HL)
                nc.scalar.copy(wh[:, j % HL, :], wraw[:, j % RAW, :]).then_inc(w_high, 1)

            def place(j, i):
                q, high = i % 2, i < 2
                if i == 0 and j >= STAT:
                    act.wait_ge(u_done, last_step_of_chunk[j - STAT] + 1)
                if i == 2:
                    wait_w_low(act, j)
                half = q if high else 1 - q
                part = wraw[:, j % RAW, :] if high else wl[:, j % HL, :].bitcast(F32)
                nc.scalar.copy(wst[half * D:(half + 1) * D, j % STAT, :, q * D:(q + 1) * D],
                               part[q * D:(q + 1) * D, :].rearrange("p (t e) -> p t e", e=D)).then_inc(w_placed, 1)

            def copy_u(s):
                act.wait_ge(u_done, s + 1)
                if pool_number[s] == 0:
                    act.wait_ge(transposed, arrival(POOL_ROWS) + 1)
                if s >= first_step_of[5]:
                    act.wait_ge(transposed, arrival(4) + 1)
                wait_summed(act, s)
                nc.scalar.copy(product_buffer(s), U[s % UB][:, :, :]).then_inc(u_copied, 1)

            def save_transposes(k):
                a = arrival(k)
                act.wait_ge(transposed, a + 1)
                nc.scalar.copy(V[:, k, :], T[:, :]).then_inc(v_saved, 1)
                if a >= 2:
                    act.wait_ge(x_in[(a - 2) % XB], 64 * ((a - 2) // XB + 1))
                nc.scalar.copy(xs[:, a % 2, 0, :], T[:, :]).then_inc(t_saved, 1)

            def save_z(bank):
                act.wait_ge(z_done, last_group_of_bank[bank] + 1)
                n = P if bank < NBANK - 1 else 96
                nc.scalar.copy(zT[0:n, z_index(bank), :], zp[0:n, :]).then_inc(z_saved, 1)

            for j in range(2):
                split_high(j)
            saved, placing = 0, [(j, i) for j in range(2) for i in range(4)]
            for what, x in order:
                if what == "T":
                    if x == NPAIR - 1:
                        for _ in range(2):
                            place(*placing.pop(0))
                    save_transposes(x)
                    if x == NPAIR - 1:
                        for _ in range(2):
                            place(*placing.pop(0))
                    if x == NPAIR - 2:
                        while placing:
                            place(*placing.pop(0))
                elif what == "R":
                    act.wait_ge(r_transposed, x + 1)
                    nc.scalar.copy(zT[:, NBANK - 1 + x, :], T[:, :]).then_inc(r_saved, 1)
                elif what == "U":
                    if x in pool_number:
                        copy_u(x)
                    if x % CHUNK_STEPS == 0 and x // CHUNK_STEPS + 2 < NCHUNK:
                        split_high(x // CHUNK_STEPS + 2)
                    if x in place_after:
                        placing += [(place_after[x], i) for i in range(4)]
                    for _ in range(PLACE_AT_ONCE):
                        if placing:
                            place(*placing.pop(0))
                    while saved < NBANK - 1 and last_group_of_bank[saved] < summed_by(x):
                        save_z(saved)
                        saved += 1
            while saved < NBANK:
                save_z(saved)
                saved += 1
            act.wait_ge(small_in, 64)
            for n in range(N1 // P):
                act.wait_ge(h_done, n + 1)
                nc.scalar.activation(h1[:, n, :], U[n // 2][:, n % 2, :], ACT.Relu,
                                     bias=b1_sb[:, n:n + 1]).then_inc(h_saved, 1)
            for n in range(N2 // P):
                act.wait_ge(h_done, N1 // P + n + 1)
                nc.scalar.activation(h2[:, n, :], U[2][:, n, :], ACT.Relu,
                                     bias=b2_sb[:, n:n + 1]).then_inc(h_saved, 1)
            act.wait_ge(y_done, 1)
            nc.scalar.copy(y_sb[0:1, :], T[0:1, :]).then_inc(y_saved, 1)

        @block.vector
        def _(dve):
            def split_low(j):
                dve.wait_ge(w_high, j + 1)
                wait_low_placed(dve, j)
                nc.vector.tensor_tensor(wl[:, j % HL, :], wraw[:, j % RAW, :], wh[:, j % HL, :].bitcast(F32),
                                        ALU.subtract).then_inc(w_low, 1)

            def split_pair(k):
                a = arrival(k)
                dve.wait_ge(t_saved, a + 1)
                nc.vector.tensor_tensor(xs[:, a % 2, 1, :], V[:, k, :], xs[:, a % 2, 0, :].bitcast(F32),
                                        ALU.subtract).then_inc(x_low, 1)

            def multiply_rows(s):
                st, i = STEPS[s], row_number[s]
                m, dm = st.pairs[0], st.pairs[1] - st.pairs[0]
                dve.wait_ge(u_done, s + 1)
                for q in range(2):
                    if i:
                        dve.wait_ge(row_summed, 2 * i - 1 + q)
                    nc.vector.tensor_tensor(row_prod[:, q, :].rearrange("p (k n) -> p k n", k=4),
                                            U[s % UB][:, q, :].rearrange("p (k n) -> p k n", k=4),
                                            rows_v[:, m:m + 3 * dm + 1:dm, 2 * (st.i % 2) + q].rearrange(
                                                "p k c d -> p k (c d)"), ALU.mult).then_inc(row_mult, 1)

            def sum_rows(s, q):
                st, i = STEPS[s], row_number[s]
                bank, at = divmod(16 * st.group + 8 * (st.i // 2), P)
                dve.wait_ge(row_mult, 2 * i + q + 1)
                nc.vector.tensor_reduce(zb[:, bank, 2 * (st.i % 2) + q, at:at + 8],
                                        row_prod[:, q, :].rearrange("p (n e) -> p n e", e=D),
                                        mybir.AxisListType.X, ALU.add).then_inc(row_summed, 1)

            def multiply(s):
                st = STEPS[s]
                names = [kind for _, _, kind in st.tiles]
                dve.wait_ge(u_done, s + 1)
                wait_summed(dve, s)
                pairs = [m for name, m in names if name == "pair"]
                if pairs:
                    dve.wait_ge(v_saved, arrival(min(pairs)) + 1)
                for name, l in names:
                    if name != "pair":
                        dve.wait_ge(vx_in, 64 * (NPAIR // 2 - l))
                p, u = product_buffer(s), U[s % UB]
                if len(names) == 1:
                    last = nc.vector.tensor_tensor(p[:, 0, :], u[:, 0, :], VX[:, 1, :], ALU.mult)
                elif names[1][0] == "even":
                    nc.vector.tensor_tensor(p[:, 0, :], u[:, 0, :], V[:, names[0][1], :], ALU.mult)
                    last = nc.vector.tensor_tensor(p[:, 1, :], u[:, 1, :], VX[:, 0, :], ALU.mult)
                else:
                    m = names[0][1]
                    last = nc.vector.tensor_tensor(p[:, :, :], u[:, :, :],
                                                   V[:, m:m + 1, :].broadcast_to([P, 2, B]), ALU.mult)
                last.then_inc(mult_done, 1)

            nc.vector.memset(sel[:, :], 0.0).then_inc(sel0, 1)
            dve.wait_ge(sel0, 1)
            for q in range(2):
                nc.vector.memset(sel[q * D:(q + 1) * D, SEL_ROWS - 2 + q:SEL_ROWS - 1 + q], 1.0).then_inc(sel_ready, 1)
            def select(k, units):
                i = PICKED.index(k)
                if 0 in units:
                    dve.wait_ge(table_in[i % 2], 48 * (i // 2 + 1))
                    if i == 0:
                        dve.wait_ge(row0_ready, 2 * len(PICKED))
                for t in units:
                    unit = units_before[k] + t
                    if unit >= UNITS:
                        dve.wait_ge(one_used, unit - UNITS + 1)
                    for c in range(2):
                        if t < PER[k][c]:
                            nc.vector.tensor_scalar(one[0:TR, unit % UNITS, c, :], idb[0:TR, i % 2, c, :],
                                                    row0[0:TR, 2 * i + c:2 * i + c + 1], float(t),
                                                    ALU.subtract, ALU.is_equal).then_inc(one_made, 1)

            waiting, to_sum = [], []
            for what, x in order:
                if what == "T":
                    if x == PICKED[0]:
                        select(x, range(UNITS))
                        split_low(0)
                        select(x, range(UNITS, max(PER[x])))
                        split_low(1)
                    elif x == PICKED[1]:
                        select(x, range(UNITS, max(PER[x])))
                        select(PICKED[2], range(UNITS))
                    elif x == PICKED[2] + 1:
                        select(PICKED[2], range(UNITS, max(PER[PICKED[2]])))
                    if x == NPAIR - 2:
                        select(PICKED[1], range(UNITS))
                    waiting.append((x, 1))
                elif what == "U":
                    if x in row_number:
                        multiply_rows(x)
                    elif x in dve_number:
                        multiply(x)
                    if to_sum:
                        sum_rows(*to_sum.pop(0))
                    if x in row_number:
                        to_sum += [(x, q) for q in range(2)]
                    if x % CHUNK_STEPS == 0 and x // CHUNK_STEPS + 2 in dve_chunks:
                        split_low(x // CHUNK_STEPS + 2)
                    waiting = [(k, n - 1) for k, n in waiting]
                due = [k for k, n in waiting if n < 0 or k >= NPAIR - 2
                       or what == "U" and x == last_step_of[STEPS[x].k]]
                for k in due:
                    split_pair(k)
                waiting = [(k, n) for k, n in waiting if k not in due]
            while to_sum:
                sum_rows(*to_sum.pop(0))

        @block.tensor
        def _(pe):
            def transposes(k):
                a = arrival(k)
                if a:
                    pe.wait_ge(t_saved, a)
                if r_before[k]:
                    pe.wait_ge(r_saved, r_before[k])
                if k in PICKED:
                    for t in range(max(PER[k])):
                        unit = units_before[k] + t
                        pe.wait_ge(one_made, made_before[k] + sum(min(t + 1, r) for r in PER[k]))
                        for c in range(2):
                            if t < PER[k][c]:
                                last = nc.tensor.matmul(T[c * D:(c + 1) * D, :],
                                                        tab[0:TR, PICKED.index(k) % 2, c, t * D:(t + 1) * D],
                                                        one[0:TR, unit % UNITS, c, :],
                                                        start=t == 0, stop=t == PER[k][c] - 1)
                        last.then_inc(one_used, 1)
                        if t == max(PER[k]) - 1:
                            pe.wait_ge(one_used, unit + 1)
                            nc.tensor.nop().then_inc(transposed, 1)
                    return
                if a == 1:
                    pe.wait_ge(ident_ready, 1)
                pe.wait_ge(rows_in[k], 2 * BT * 16)
                for q in range(BT):
                    last = nc.tensor.transpose(T[:, q * P:(q + 1) * P],
                                               rows_v[:, k, q, :, :].rearrange("p c d -> p (c d)"), ident[:, :])
                last.then_inc(transposed, 1)

            def products(s):
                st = STEPS[s]
                k, a, chunk = st.k, arrival(st.k), st.w // CHUNK_STEPS
                pe.wait_ge(w_placed, 4 * (chunk + 1))
                if s == first_step_of[k]:
                    pe.wait_ge(x_in[a % XB], 64 * (a // XB + 1))
                if s >= UB:
                    wait_u_read(pe, s - UB)
                if st.group is None:
                    for c, (centre, _, _) in enumerate(st.tiles):
                        slot = 2 * (st.w % CHUNK_STEPS) + c
                        for part in range(2):
                            last = nc.tensor.matmul(U[s % UB][:, c, :], wst[:, chunk % STAT, slot, :],
                                                    X[:, a % XB, centre % 2, part, :], start=part == 0, stop=part == 1)
                else:
                    c = st.i // 2
                    first = 2 * ((st.w - st.i) % CHUNK_STEPS) + c
                    for i in range(2):
                        q = 2 * (st.i % 2) + i
                        for part in range(2):
                            last = nc.tensor.matmul(U[s % UB][:, i, :], X[:, a % XB, c, part, q * P:(q + 1) * P],
                                                    wst[:, chunk % STAT, first:first + 7:2, :],
                                                    start=part == 0, stop=part == 1)
                last.then_inc(u_done, 1)

            def transpose_rows(bank):
                pe.wait_ge(row_summed, 2 * len(row_steps) // NROWBANK * (bank + 1))
                pe.wait_ge(t_saved, t_before[bank])
                if bank:
                    pe.wait_ge(r_saved, bank)
                for q in range(BT):
                    last = nc.tensor.transpose(T[:, q * P:(q + 1) * P], zb[:, bank, q, :], ident[:, :])
                last.then_inc(r_transposed, 1)

            t_before, r_before, n_t, n_r = {}, {}, 0, 0
            for what, x in order:
                if what == "T":
                    r_before[x] = n_r
                    n_t += 1
                elif what == "R":
                    t_before[x] = n_t
                    n_r += 1

            def sums(g):
                tiles = GROUPS[g]
                bank = tiles[0] // BANK_TILES
                of_dve = [dve_number[step_of_tile[n]] for n in tiles if step_of_tile[n] in dve_number]
                of_pool = [pool_number[step_of_tile[n]] for n in tiles if step_of_tile[n] in pool_number]
                if of_dve:
                    pe.wait_ge(mult_done, max(of_dve) + 1)
                if of_pool:
                    pe.wait_ge(pool_done, max(of_pool) + 1)
                if g == 0:
                    pe.wait_ge(sel_ready, 2)
                if tiles[0] % BANK_TILES == 0 and bank:
                    pe.wait_ge(z_saved, bank)
                for n in tiles:
                    _, q, r = z_place(n)
                    s, c = TILES[n]
                    of_quadrant = [m for m in range(bank * BANK_TILES, min(NT, (bank + 1) * BANK_TILES))
                                   if z_place(m)[1] == q]
                    last = nc.tensor.matmul(zp[SEL_ROWS * q:SEL_ROWS * (q + 1), :],
                                            sel[:, SEL_ROWS - 2 - 2 * r:2 * SEL_ROWS - 2 - 2 * r],
                                            product_buffer(s)[:, c, :], start=n == of_quadrant[0],
                                            stop=n == of_quadrant[-1])
                last.then_inc(z_done, 1)

            g = 0
            for what, x in order:
                if what == "T":
                    transposes(x)
                elif what == "U":
                    products(x)
                    while g < summed_by(x):
                        sums(g)
                        g += 1
                elif what == "R":
                    transpose_rows(x)
            while g < len(GROUPS):
                sums(g)
                g += 1

            pe.wait_ge(w_mlp_in, 16 * 7)
            pe.wait_ge(small_in, 64)
            pe.wait_ge(z_saved, NBANK - 1)
            pe.wait_ge(r_saved, NROWBANK)
            for s in range(NS - UB, NS):
                wait_u_read(pe, s)
            for n in range(N1 // P):
                for b in range(NZ - 1):
                    nc.tensor.matmul(U[n // 2][:, n % 2, :], w1_sb[b][:, n * P:(n + 1) * P], zT[:, b, :],
                                     start=b == 0, stop=False)
            pe.wait_ge(z_saved, NBANK)
            for n in range(N1 // P):
                nc.tensor.matmul(U[n // 2][:, n % 2, :], w1_end[0:96 + ND, n * P:(n + 1) * P],
                                 zT[0:96 + ND, NZ - 1, :], start=False, stop=True).then_inc(h_done, 1)
            for n in range(N2 // P):
                for b in range(N1 // P):
                    if n == 0:
                        pe.wait_ge(h_saved, b + 1)
                    last = nc.tensor.matmul(U[2][:, n, :], w2_sb[:, b, n * P:(n + 1) * P], h1[:, b, :],
                                            start=b == 0, stop=b == N1 // P - 1)
                last.then_inc(h_done, 1)
            pe.wait_ge(t_saved, NPAIR)
            for b in range(N2 // P):
                pe.wait_ge(h_saved, N1 // P + b + 1)
                last = nc.tensor.matmul(T[0:1, :], w3_sb[:, b:b + 1], h2[:, b, :], start=b == 0,
                                        stop=b == N2 // P - 1)
            last.then_inc(y_done, 1)


def laid_out(inputs):
    W = np.asarray(inputs["L0_rec_W"])
    number = {pair: n for n, pair in enumerate(zip(*np.triu_indices(F, k=1)))}
    zeros = np.zeros((D, D), W.dtype)
    w = [[[zeros, zeros] for _ in range(SLOTS)] for _ in range(NCHUNK)]
    product = {}
    for st in WEIGHTS:
        for c, (centre, partners, _) in enumerate(st.tiles):
            for q, j in enumerate(partners):
                p = number[(min(centre, j), max(centre, j))]
                w[st.w // CHUNK_STEPS][2 * (st.w % CHUNK_STEPS) + c][q] = W[p] if centre < j else W[p].T
                product[st.w, c, q] = p
    w_pairs = np.array(w).transpose(0, 2, 3, 1, 4).reshape(NCHUNK, P, SLOTS * D)
    W1 = np.asarray(inputs["W_top1"])
    main = np.zeros((NZ - 1, P), np.int64)
    last = np.zeros((3, 2 * LAST // 3), np.int64)
    for n, (s, c) in enumerate(TILES):
        bank, q, r = z_place(n)
        for half in range(2):
            if bank < NBANK - 1:
                main[bank, SEL_ROWS * q + 2 * r + half] = product[STEPS[s].w, c, half]
            else:
                last[q, 2 * r + half] = product[STEPS[s].w, c, half]
    for st in WEIGHTS:
        if st.group is not None:
            for c in range(2):
                for half in range(2):
                    bank, at = divmod(16 * st.group + 8 * c + 2 * st.i + half, P)
                    main[NBANK - 1 + bank, at] = product[st.w, c, half]
    W2 = np.asarray(inputs["W_top2"])
    return {
        "dense_t": np.asarray(inputs["dense_ctx"]).T,
        "ids": np.asarray(inputs["ids"]),
        "ids_t": np.asarray(inputs["ids"]).T,
        **{f"tbl_{f}": np.asarray(inputs[f"tbl_{f}"]) for f in range(F)},
        "w_pairs": w_pairs,
        "w1_main": W1[main].transpose(1, 0, 2),
        "w1_last": W1[last],
        "w1_dense": W1[F * (F - 1) // 2:],
        "b1": np.asarray(inputs["b_top1"]).reshape(N1 // P, P).T,
        "w2": W2.reshape(N1 // P, P, N2).transpose(1, 0, 2),
        "b2": np.asarray(inputs["b_top2"]).reshape(N2 // P, P).T,
        "w3": np.asarray(inputs["W_top3"]).reshape(N2 // P, P).T,
    }


def kernel(**inputs):
    import concourse.bacc as bacc
    from concourse.bass_utils import run_bass_kernel_spmd

    nc = bacc.Bacc("TRN2", target_bir_lowering=False, num_devices=1)
    arrays, aps = {}, {}
    for name, a in laid_out(inputs).items():
        a = np.ascontiguousarray(a)
        arrays[f"in_{name}"] = a
        aps[name] = nc.dram_tensor(f"in_{name}", a.shape, mybir.dt.from_np(a.dtype), kind="ExternalInput").ap()
    out = nc.dram_tensor("out_y", (B, 1), F32, kind="ExternalOutput").ap()
    tables = [aps.pop(f"tbl_{f}") for f in range(F)]
    build(nc, tables=tables, out=out, **aps)
    r = run_bass_kernel_spmd(nc, [arrays], core_ids=[0])
    return r.results[0]["out_y"]
```
